# Optimizing a Trainium2 kernel written in Bass

```python
import numpy as np
import jax
import jax.numpy as jnp

def _softmax(x, axis=-1):
    return jax.nn.softmax(x, axis=axis)

def _gelu(x):
    return jax.nn.gelu(x, approximate=True)

def _silu(x):
    return jax.nn.silu(x)

def _sigmoid(x):
    return jax.nn.sigmoid(x)

def _layernorm(x, axis=-1, eps=1e-05):
    m = jnp.mean(x, axis=axis, keepdims=True)
    v = jnp.var(x, axis=axis, keepdims=True)
    return (x - m) / jnp.sqrt(v + eps)

def _scatter_add(tgt, idx, src, axis=0):
    return tgt.at[idx].add(src)

def _segment_sum(src, seg, n):
    return jax.ops.segment_sum(src, seg, n)
kernel_name = 'mk_audio_tower_d2_tok_audfeat512_r4_b373bf'

def setup_inputs(seed: int=0):
    np.random.seed(seed)
    _w = jnp.asarray

    def _rec_inputs():
        import jax
        import jax.numpy as jnp
        _rk = jax.random.key(seed)
        x = -6.41493e-05 + 1.00002 * jax.random.normal(jax.random.fold_in(_rk, 1), (64, 256, 80), jnp.float32)
        return x
    x = _rec_inputs()

    def _L0_tok_setup():
        import jax, jax.numpy as jnp
        import numpy as np
        CTX = np.array([-2, -1, 0, 1, 2])
        STRIDE = 1
        EPS = 1e-05
        key = jax.random.key(seed)
        k1, k2, k3 = jax.random.split(key, 3)
        B, L, D = (64, 500, 80)
        O, K = (128, D * len(CTX))
        x = jax.random.normal(k1, (B, L, D), dtype=jnp.float32)
        W = jax.random.normal(k2, (O, K), dtype=jnp.float32) * (1.0 / np.sqrt(K))
        b = jax.random.normal(k3, (O,), dtype=jnp.float32) * 0.01
        gamma = jnp.ones((O,), dtype=jnp.float32)
        beta = jnp.zeros((O,), dtype=jnp.float32)
        return {'x': x, 'W': W, 'b': b, 'gamma': gamma, 'beta': beta}
    _L0_tok_all = _L0_tok_setup()
    _L0_tok_in = {k: v for k, v in _L0_tok_all.items() if k in ('W', 'b', 'gamma', 'beta')}
    del _L0_tok_all

    def _L0_attn_setup():
        import jax, jax.numpy as jnp
        import numpy as np
        D_MODEL = 128
        N_HEADS = 8
        HEAD_DIM = D_MODEL // N_HEADS
        WINDOW = 5

        def _ocr_pattern_mask(S, dtype):
            idx = jnp.arange(S)
            band = jnp.abs(idx[:, None] - idx[None, :]) <= WINDOW
            return jnp.where(band, jnp.asarray(0.1, dtype), jnp.asarray(0.0, dtype))
        key = jax.random.key(seed)
        ks = jax.random.split(key, 12)
        B, S = (4, 512)
        x = jax.random.normal(ks[0], (B, S, D_MODEL), dtype=jnp.float32)
        ocr_context = jax.random.randint(ks[1], (B, S), 0, 100, dtype=jnp.int64)
        scale = 0.02
        Wq = jax.random.normal(ks[2], (D_MODEL, D_MODEL), dtype=jnp.float32) * scale
        bq = jax.random.normal(ks[3], (D_MODEL,), dtype=jnp.float32) * scale
        Wk = jax.random.normal(ks[4], (D_MODEL, D_MODEL), dtype=jnp.float32) * scale
        bk = jax.random.normal(ks[5], (D_MODEL,), dtype=jnp.float32) * scale
        Wv = jax.random.normal(ks[6], (D_MODEL, D_MODEL), dtype=jnp.float32) * scale
        bv = jax.random.normal(ks[7], (D_MODEL,), dtype=jnp.float32) * scale
        Wo = jax.random.normal(ks[8], (D_MODEL, D_MODEL), dtype=jnp.float32) * scale
        bo = jax.random.normal(ks[9], (D_MODEL,), dtype=jnp.float32) * scale
        ocr_bias = jax.random.normal(ks[10], (D_MODEL,), dtype=jnp.float32)
        return {'x': x, 'ocr_context': ocr_context, 'Wq': Wq, 'bq': bq, 'Wk': Wk, 'bk': bk, 'Wv': Wv, 'bv': bv, 'Wo': Wo, 'bo': bo, 'ocr_bias': ocr_bias}
    _L0_attn_all = _L0_attn_setup()
    _L0_attn_in = {k: v for k, v in _L0_attn_all.items() if k in ('ocr_context', 'Wq', 'bq', 'Wk', 'bk', 'Wv', 'bv', 'Wo', 'bo', 'ocr_bias')}
    del _L0_attn_all

    def _L0_ffn_setup():
        import jax, jax.numpy as jnp
        import numpy as np
        B, S, D, H, E = (4, 512, 128, 256, 8)
        key = jax.random.key(seed)
        ks = jax.random.split(key, 4)
        x = jax.random.normal(ks[0], (B, S, D), jnp.float32)
        Wr = jax.random.normal(ks[1], (E, D), jnp.float32) * 0.02
        br = jnp.zeros((E,), jnp.float32)
        W1 = jax.random.normal(ks[2], (E, D, H), jnp.float32) * 0.02
        b1 = jnp.zeros((E, H), jnp.float32)
        W2 = jax.random.normal(ks[3], (E, H, D), jnp.float32) * 0.02
        b2 = jnp.zeros((E, D), jnp.float32)
        return {'x': x, 'Wr': Wr, 'br': br, 'W1': W1, 'b1': b1, 'W2': W2, 'b2': b2}
    _L0_ffn_all = _L0_ffn_setup()
    _L0_ffn_in = {k: v for k, v in _L0_ffn_all.items() if k in ('Wr', 'br', 'W1', 'b1', 'W2', 'b2')}
    del _L0_ffn_all

    def _L1_attn_setup():
        import jax, jax.numpy as jnp
        import numpy as np
        D_MODEL, N_HEADS, D_VALUE = (128, 8, 64)
        D_HEAD = D_MODEL // N_HEADS

        def _elu_feature_map(t):
            return jax.nn.elu(t) + 1.0
        key = jax.random.key(seed)
        ks = jax.random.split(key, 5)
        B, T = (2, 512)
        x = jax.random.normal(ks[0], (B, T, D_MODEL), dtype=jnp.float32)
        scale = 0.02
        W_q = jax.random.normal(ks[1], (N_HEADS * D_HEAD, D_MODEL), dtype=jnp.float32) * scale
        W_k = jax.random.normal(ks[2], (N_HEADS * D_HEAD, D_MODEL), dtype=jnp.float32) * scale
        W_v = jax.random.normal(ks[3], (N_HEADS * D_VALUE, D_MODEL), dtype=jnp.float32) * scale
        W_out = jax.random.normal(ks[4], (D_MODEL, N_HEADS * D_VALUE), dtype=jnp.float32) * scale
        return {'x': x, 'W_q': W_q, 'W_k': W_k, 'W_v': W_v, 'W_out': W_out}
    _L1_attn_all = _L1_attn_setup()
    _L1_attn_in = {k: v for k, v in _L1_attn_all.items() if k in ('W_q', 'W_k', 'W_v', 'W_out')}
    del _L1_attn_all

    def _L1_ffn_setup():
        import jax, jax.numpy as jnp
        import numpy as np
        B, N, DIM = (1, 512, 128)
        DH, H = (64, 8)
        E, FF = (8, 512)

        def _layernorm(x, g, b, eps=1e-05):
            mu = jnp.mean(x, axis=-1, keepdims=True)
            var = jnp.mean(jnp.square(x - mu), axis=-1, keepdims=True)
            return (x - mu) * jax.lax.rsqrt(var + eps) * g + b

        def _l2norm(x, eps=1e-12):
            return x / jnp.sqrt(jnp.sum(jnp.square(x), axis=-1, keepdims=True) + eps)
        key = jax.random.key(seed)
        ks = jax.random.split(key, 12)
        g = lambda k, shape: jax.random.normal(k, shape, jnp.float32) * 0.02
        return {'x': jax.random.normal(ks[0], (B, N, DIM), jnp.float32), 'ln_g': jnp.ones((DIM,), jnp.float32), 'ln_b': jnp.zeros((DIM,), jnp.float32), 'Wq': g(ks[1], (DIM, DIM)), 'Wk': g(ks[2], (DIM, DIM)), 'Wv': g(ks[3], (DIM, DIM)), 'Wo': g(ks[4], (DIM, DIM)), 'qn_g': jnp.ones((DH,), jnp.float32), 'kn_g': jnp.ones((DH,), jnp.float32), 'gate_W': g(ks[5], (DIM, E)), 'gate_b': jnp.zeros((E,), jnp.float32), 'W1': g(ks[6], (E, DIM, FF)), 'b1': jnp.zeros((E, FF), jnp.float32), 'W2': g(ks[7], (E, FF, DIM)), 'b2': jnp.zeros((E, DIM), jnp.float32)}
    _L1_ffn_all = _L1_ffn_setup()
    _L1_ffn_in = {k: v for k, v in _L1_ffn_all.items() if k in ('ln_g', 'ln_b', 'Wq', 'Wk', 'Wv', 'Wo', 'qn_g', 'kn_g', 'gate_W', 'gate_b', 'W1', 'b1', 'W2', 'b2')}
    del _L1_ffn_all
    return {'x': x, 'L0_tok_W': _L0_tok_in['W'], 'L0_tok_b': _L0_tok_in['b'], 'L0_tok_gamma': _L0_tok_in['gamma'], 'L0_tok_beta': _L0_tok_in['beta'], 'L0_attn_ocr_context': _L0_attn_in['ocr_context'], 'L0_attn_Wq': _L0_attn_in['Wq'], 'L0_attn_bq': _L0_attn_in['bq'], 'L0_attn_Wk': _L0_attn_in['Wk'], 'L0_attn_bk': _L0_attn_in['bk'], 'L0_attn_Wv': _L0_attn_in['Wv'], 'L0_attn_bv': _L0_attn_in['bv'], 'L0_attn_Wo': _L0_attn_in['Wo'], 'L0_attn_bo': _L0_attn_in['bo'], 'L0_attn_ocr_bias': _L0_attn_in['ocr_bias'], 'L0_ffn_Wr': _L0_ffn_in['Wr'], 'L0_ffn_br': _L0_ffn_in['br'], 'L0_ffn_W1': _L0_ffn_in['W1'], 'L0_ffn_b1': _L0_ffn_in['b1'], 'L0_ffn_W2': _L0_ffn_in['W2'], 'L0_ffn_b2': _L0_ffn_in['b2'], 'L1_attn_W_q': _L1_attn_in['W_q'], 'L1_attn_W_k': _L1_attn_in['W_k'], 'L1_attn_W_v': _L1_attn_in['W_v'], 'L1_attn_W_out': _L1_attn_in['W_out'], 'L1_ffn_ln_g': _L1_ffn_in['ln_g'], 'L1_ffn_ln_b': _L1_ffn_in['ln_b'], 'L1_ffn_Wq': _L1_ffn_in['Wq'], 'L1_ffn_Wk': _L1_ffn_in['Wk'], 'L1_ffn_Wv': _L1_ffn_in['Wv'], 'L1_ffn_Wo': _L1_ffn_in['Wo'], 'L1_ffn_qn_g': _L1_ffn_in['qn_g'], 'L1_ffn_kn_g': _L1_ffn_in['kn_g'], 'L1_ffn_gate_W': _L1_ffn_in['gate_W'], 'L1_ffn_gate_b': _L1_ffn_in['gate_b'], 'L1_ffn_W1': _L1_ffn_in['W1'], 'L1_ffn_b1': _L1_ffn_in['b1'], 'L1_ffn_W2': _L1_ffn_in['W2'], 'L1_ffn_b2': _L1_ffn_in['b2']}

def reference(x, L0_tok_W, L0_tok_b, L0_tok_gamma, L0_tok_beta, L0_attn_ocr_context, L0_attn_Wq, L0_attn_bq, L0_attn_Wk, L0_attn_bk, L0_attn_Wv, L0_attn_bv, L0_attn_Wo, L0_attn_bo, L0_attn_ocr_bias, L0_ffn_Wr, L0_ffn_br, L0_ffn_W1, L0_ffn_b1, L0_ffn_W2, L0_ffn_b2, L1_attn_W_q, L1_attn_W_k, L1_attn_W_v, L1_attn_W_out, L1_ffn_ln_g, L1_ffn_ln_b, L1_ffn_Wq, L1_ffn_Wk, L1_ffn_Wv, L1_ffn_Wo, L1_ffn_qn_g, L1_ffn_kn_g, L1_ffn_gate_W, L1_ffn_gate_b, L1_ffn_W1, L1_ffn_b1, L1_ffn_W2, L1_ffn_b2):
    import jax
    import jax.numpy as jnp

    def _L0_tok_ref(x, W, b, gamma, beta):
        import jax, jax.numpy as jnp
        import numpy as np
        CTX = np.array([-2, -1, 0, 1, 2])
        STRIDE = 1
        EPS = 1e-05
        B, L, D = x.shape
        ctx = jnp.asarray(CTX)
        vi = jnp.arange(-int(CTX.min()), L - int(CTX.max()), STRIDE)
        idx = vi[:, None] + ctx[None, :]
        g = x[:, idx, :]
        g = g.reshape(B, vi.shape[0], -1)
        y = jnp.einsum('blk,ok->blo', g, W) + b
        y = jax.nn.relu(y)
        mean = jnp.mean(y, axis=(0, 1))
        var = jnp.var(y, axis=(0, 1))
        return (y - mean) * jax.lax.rsqrt(var + EPS) * gamma + beta

    def _L0_attn_ref(x, ocr_context, Wq, bq, Wk, bk, Wv, bv, Wo, bo, ocr_bias):
        import jax, jax.numpy as jnp
        import numpy as np
        D_MODEL = 128
        N_HEADS = 8
        HEAD_DIM = D_MODEL // N_HEADS
        WINDOW = 5

        def _ocr_pattern_mask(S, dtype):
            idx = jnp.arange(S)
            band = jnp.abs(idx[:, None] - idx[None, :]) <= WINDOW
            return jnp.where(band, jnp.asarray(0.1, dtype), jnp.asarray(0.0, dtype))
        B, S, D = x.shape
        H, hd = (N_HEADS, HEAD_DIM)
        q = (x @ Wq.T + bq).reshape(B, S, H, hd)
        k = (x @ Wk.T + bk).reshape(B, S, H, hd)
        v = (x @ Wv.T + bv).reshape(B, S, H, hd)
        q = q + ocr_bias.reshape(H, hd)
        scores = jnp.einsum('bqhd,bkhd->bhqk', q, k) / np.sqrt(hd).astype(x.dtype)
        scores = scores + _ocr_pattern_mask(S, scores.dtype)
        attn = jax.nn.softmax(scores, axis=-1)
        out = jnp.einsum('bhqk,bkhd->bqhd', attn, v).reshape(B, S, D)
        return out @ Wo.T + bo

    def _L0_ffn_ref(x, Wr, br, W1, b1, W2, b2):
        import jax, jax.numpy as jnp
        import numpy as np
        B, S, D, H, E = (4, 512, 128, 256, 8)
        b, s, d = x.shape
        n = b * s
        e = Wr.shape[0]
        xf = x.reshape(n, d)
        logits = xf @ Wr.T + br
        probs = jax.nn.softmax(logits, axis=-1)
        top2_prob, top2_idx = jax.lax.top_k(probs, 2)
        comb = jnp.zeros((n, e), x.dtype).at[jnp.arange(n)[:, None], top2_idx].add(top2_prob)
        h = jax.nn.gelu(jnp.einsum('nd,edh->enh', xf, W1) + b1[:, None, :], approximate=False)
        o = jnp.einsum('enh,ehd->end', h, W2) + b2[:, None, :]
        y = jnp.einsum('ne,end->nd', comb, o)
        return y.reshape(b, s, d)

    def _L1_attn_ref(x, W_q, W_k, W_v, W_out):
        import jax, jax.numpy as jnp
        import numpy as np
        D_MODEL, N_HEADS, D_VALUE = (128, 8, 64)
        D_HEAD = D_MODEL // N_HEADS

        def _elu_feature_map(t):
            return jax.nn.elu(t) + 1.0
        B, T, D = x.shape
        H, dh, dv = (N_HEADS, D_HEAD, D_VALUE)
        Q = _elu_feature_map((x @ W_q.T).reshape(B, T, H, dh)).transpose(0, 2, 1, 3)
        K = _elu_feature_map((x @ W_k.T).reshape(B, T, H, dh)).transpose(0, 2, 1, 3)
        V = (x @ W_v.T).reshape(B, T, H, dv).transpose(0, 2, 1, 3)
        KV = jnp.einsum('bhti,bhtj->bhtij', K, V)
        S = jnp.cumsum(KV, axis=2)
        z = jnp.cumsum(K, axis=2)
        num = jnp.einsum('bhti,bhtij->bhtj', Q, S)
        den = jnp.maximum(jnp.einsum('bhti,bhti->bht', Q, z), 1e-06)[..., None]
        out = (num / den).transpose(0, 2, 1, 3).reshape(B, T, H * dv)
        return out @ W_out.T

    def _L1_ffn_ref(x, ln_g, ln_b, Wq, Wk, Wv, Wo, qn_g, kn_g, gate_W, gate_b, W1, b1, W2, b2):
        import jax, jax.numpy as jnp
        import numpy as np
        B, N, DIM = (1, 512, 128)
        DH, H = (64, 8)
        E, FF = (8, 512)

        def _layernorm(x, g, b, eps=1e-05):
            mu = jnp.mean(x, axis=-1, keepdims=True)
            var = jnp.mean(jnp.square(x - mu), axis=-1, keepdims=True)
            return (x - mu) * jax.lax.rsqrt(var + eps) * g + b

        def _l2norm(x, eps=1e-12):
            return x / jnp.sqrt(jnp.sum(jnp.square(x), axis=-1, keepdims=True) + eps)
        b, n, d = x.shape
        dh = qn_g.shape[0]
        h = d // dh
        hx = _layernorm(x, ln_g, ln_b)
        q = (hx @ Wq).reshape(b, n, h, dh).transpose(0, 2, 1, 3)
        k = (hx @ Wk).reshape(b, n, h, dh).transpose(0, 2, 1, 3)
        v = (hx @ Wv).reshape(b, n, h, dh).transpose(0, 2, 1, 3)
        scale = jnp.sqrt(jnp.float32(dh))
        q = _l2norm(q) * scale * qn_g
        k = _l2norm(k) * scale * kn_g
        scores = jnp.einsum('bhqd,bhkd->bhqk', q, k) * dh ** (-0.5)
        causal = jnp.tril(jnp.ones((n, n), bool))
        scores = jnp.where(causal, scores, jnp.finfo(scores.dtype).min)
        attn = jax.nn.softmax(scores, axis=-1)
        o = jnp.einsum('bhqk,bhkd->bhqd', attn, v)
        y = o.transpose(0, 2, 1, 3).reshape(b, n, d) @ Wo
        gate = jax.nn.softmax(y @ gate_W + gate_b, axis=-1)
        hid = jax.nn.gelu(jnp.einsum('bnd,edf->bnef', y, W1) + b1)
        eo = jnp.einsum('bnef,efd->bned', hid, W2) + b2
        out = jnp.einsum('bned,bne->bnd', eo, gate)
        return out
    h = _L0_tok_ref(x, L0_tok_W, L0_tok_b, L0_tok_gamma, L0_tok_beta)
    h = h + _L0_attn_ref(_layernorm(h, axis=-1), L0_attn_ocr_context, L0_attn_Wq, L0_attn_bq, L0_attn_Wk, L0_attn_bk, L0_attn_Wv, L0_attn_bv, L0_attn_Wo, L0_attn_bo, L0_attn_ocr_bias)
    h = h + _L0_ffn_ref(_layernorm(h, axis=-1), L0_ffn_Wr, L0_ffn_br, L0_ffn_W1, L0_ffn_b1, L0_ffn_W2, L0_ffn_b2)
    h = h + _L1_attn_ref(_layernorm(h, axis=-1), L1_attn_W_q, L1_attn_W_k, L1_attn_W_v, L1_attn_W_out)
    h = h + _L1_ffn_ref(_layernorm(h, axis=-1), L1_ffn_ln_g, L1_ffn_ln_b, L1_ffn_Wq, L1_ffn_Wk, L1_ffn_Wv, L1_ffn_Wo, L1_ffn_qn_g, L1_ffn_kn_g, L1_ffn_gate_W, L1_ffn_gate_b, L1_ffn_W1, L1_ffn_b1, L1_ffn_W2, L1_ffn_b2)
    return h

_drawn_inputs = setup_inputs


def setup_inputs(seed=0):
    import zlib

    import numpy as np

    out = dict(_drawn_inputs(seed))
    spreads = {'L0_tok_gamma': (1.0, 0.2),
     'L0_tok_beta': (0.0, 0.1),
     'L0_ffn_br': (0.0, 0.418),
     'L0_ffn_b1': (0.0, 0.8),
     'L0_ffn_b2': (0.0, 0.377),
     'L1_ffn_ln_g': (1.0, 0.6),
     'L1_ffn_ln_b': (0.0, 0.8),
     'L1_ffn_qn_g': (1.0, 0.6),
     'L1_ffn_kn_g': (1.0, 0.6),
     'L1_ffn_gate_b': (0.0, 0.8),
     'L1_ffn_b1': (0.0, 0.8),
     'L1_ffn_b2': (0.0, 0.8)}
    factors = {'L0_tok_b': 8.0,
     'L0_attn_Wq': 8.0,
     'L0_attn_bq': 8.0,
     'L0_attn_Wk': 8.0,
     'L0_attn_bk': 64.0,
     'L0_attn_Wv': 8.0,
     'L0_attn_bv': 8.0,
     'L0_attn_Wo': 8.0,
     'L0_attn_ocr_bias': 8.0,
     'L0_ffn_Wr': 2.931,
     'L0_ffn_W1': 6.59,
     'L0_ffn_W2': 6.02,
     'L1_attn_W_q': 25.708,
     'L1_attn_W_k': 8.0,
     'L1_attn_W_v': 3.322,
     'L1_attn_W_out': 3.401,
     'L1_ffn_Wq': 8.0,
     'L1_ffn_Wk': 8.0,
     'L1_ffn_Wv': 8.0,
     'L1_ffn_Wo': 8.0,
     'L1_ffn_gate_W': 8.0,
     'L1_ffn_W1': 8.0,
     'L1_ffn_W2': 7.182,
     'L0_attn_bo': 2.964}
    for name, (base, spread) in spreads.items():
        noise = np.random.default_rng([zlib.crc32(name.encode()), seed]).standard_normal(out[name].shape)
        drawn = base * np.exp(spread * noise) if base else spread * noise
        out[name] = jnp.asarray(drawn.astype(out[name].dtype))
    for name, factor in factors.items():
        out[name] = (out[name] * factor).astype(out[name].dtype)
    return out
```

```python
from contextlib import ExitStack, contextmanager

import numpy as np

import concourse.bass as bass
from concourse import mybir

ALU = mybir.AluOpType
ACT = mybir.ActivationFunctionType
AX = mybir.AxisListType
F32 = mybir.dt.float32
F16 = mybir.dt.float16

BATCH, LENGTH, CHANNELS = 64, 256, 80
TAPS = 5
SEQ = LENGTH - TAPS + 1
D = 128
TILE = SEQ // 2
TILES = 4
TOK = TILES * TILE
PAIRS = BATCH // 2
HEADS, HEAD = 8, 16
GROUPS = HEADS // 2
LIN_VALUE = 64
HEADS2, HEAD2 = 2, 64
EXPERTS = 8
CHUNKS0, CHUNKS1 = 2, 4
EPS = 1e-5
BAND, BAND_WIDTH = 5, 131
LAG = 3

WIDTHS = [("tok", TAPS * D), ("wq0", D), ("wk0", D), ("wv0", D), ("wo0", D),
          ("wq1", D), ("wk1", D), ("wv1", HEADS * LIN_VALUE), ("wo1", HEADS * LIN_VALUE),
          ("wqkv2", 3 * D), ("wo2", D), ("gate0", EXPERTS), ("gate1", EXPERTS),
          ("up0", EXPERTS * CHUNKS0 * 128), ("down0", EXPERTS * CHUNKS0 * D),
          ("up1", EXPERTS * CHUNKS1 * 128), ("down1", EXPERTS * CHUNKS1 * D)]
COL, NCOL = {}, 0
for _name, _width in WIDTHS:
    COL[_name] = NCOL
    NCOL += _width
PIECES = 8
PIECE = NCOL // PIECES
assert PIECE * PIECES == NCOL and NCOL <= PAIRS * TOK
V_TOKB, V_GAMMA, V_BETA, V_BQ, V_OCR, V_BK, V_LNG, V_LNB, V_QN, V_KN = range(10)
V_B0 = 10
V_B1 = V_B0 + EXPERTS * CHUNKS0
NVEC = V_B1 + EXPERTS * CHUNKS1
R_BV, R_BO, R_G0, R_G1 = 0, D, 2 * D, 2 * D + EXPERTS
NROW = 2 * D + 2 * EXPERTS

START = 4


class Count:

    def __init__(self, per_round, offset):
        self.per_round, self.offset = per_round, offset

    def __add__(self, other):
        if isinstance(other, Count):
            return Count(self.per_round + other.per_round, self.offset + other.offset)
        return Count(self.per_round, self.offset + other)

    __radd__ = __add__

    def __sub__(self, other):
        return self + -1 * other

    def __mul__(self, factor):
        return Count(self.per_round * factor, self.offset * factor)

    __rmul__ = __mul__


class Counter:

    def __init__(self, engine, name):
        self.engine, self.round, self.multiples = engine, None, {}
        self.value = engine.alloc_register(name)

    @contextmanager
    def loop(self, rounds):
        with self.engine.Fori(0, rounds) as k:
            self.round, self.multiples = k, {}
            yield Count(1, 0)
            self.round = None

    def plain(self, count):
        if not isinstance(count, Count):
            return count
        if count.per_round == 0:
            return count.offset
        if count.per_round not in self.multiples:
            self.multiples[count.per_round] = self.engine.snap(self.round * count.per_round)
        self.engine.reg_add(self.value, self.multiples[count.per_round], count.offset)
        return self.value

    def __call__(self, count):
        return self.plain(count + START)

    def index(self, count):
        if not isinstance(count, Count) or count.per_round == 0:
            return count.offset if isinstance(count, Count) else count
        return self.round * count.per_round + count.offset


def phase_of(kind, k, x):
    p = k * 2 + x
    if kind == "A0":
        before0, before1 = p, k * 2
    else:
        before0, before1 = k * 2 + 2, p
    return p, before0 + before1, before0 * 3 + before1 * 7


def chunks_before(kind, k, x):
    p = k * 2 + x
    if kind == 0:
        before0, before1 = p, k * 2
    else:
        before0, before1 = k * 2 + 2, p
    return (before0 + before1) * 8, before0 * 16 + before1 * 32


def weave(ffn, attention, ffn_steps, attention_steps):
    done = 0
    for i in range(ffn_steps):
        next(ffn)
        while done * ffn_steps < (i + 1) * attention_steps:
            next(attention)
            done += 1
    assert next(ffn, "end") == "end" and next(attention, "end") == "end"


FFN_STEPS = (EXPERTS * CHUNKS0 + LAG, EXPERTS * CHUNKS1 + LAG)
A0_STEPS, A1_STEPS = 23, 31


def program(nc, x_dram, w_dram, vec_dram, row_dram, b2_dram, out_dram):
    with ExitStack() as ctx:
        def sb(name, shape, dt=F32):
            return ctx.enter_context(nc.sbuf_tensor(name, shape, dt))

        def sem(name):
            return ctx.enter_context(nc.semaphore(name))

        y_all = sb("y_all", [128, PAIRS * TOK])
        w_hi = sb("w_hi", [128, NCOL], F16)
        w_lo = sb("w_lo", [128, NCOL], F16)
        vec = sb("vec", [128, NVEC])
        rows = sb("rows", [128, NROW])
        b2 = sb("b2", [EXPERTS, 2, D])
        ident = sb("ident", [128, 128])
        ident16 = sb("ident16", [128, 128], F16)
        pick_q_hi = sb("pick_q_hi", [128, GROUPS, 128], F16)
        pick_q_lo = sb("pick_q_lo", [128, GROUPS, 128], F16)
        pick_k_hi = sb("pick_k_hi", [128, GROUPS, 128], F16)
        pick_k_lo = sb("pick_k_lo", [128, GROUPS, 128], F16)
        one_row = sb("one_row", [128, 1])
        band = sb("band", [128, 2, BAND_WIDTH])
        causal = sb("causal", [128, 3, TILE])
        causal_add = sb("causal_add", [128, 3, TILE])
        earlier = sb("earlier", [128, EXPERTS, EXPERTS])
        minus_half = sb("minus_half", [128, 16])
        q_bias = sb("q_bias", [128, 1])
        qk_gain = sb("qk_gain", [128, 1])
        bn = sb("bn", [128, 2])
        bn_var = sb("bn_var", [128, 1])
        bn_rstd = sb("bn_rstd", [128, 1])
        bn_scale = sb("bn_scale", [128, 1])
        bn_shift = sb("bn_shift", [128, 1])
        h = sb("h", [128, 2, TILES, D])
        xf_hi = sb("xf_hi", [128, 2, 512], F16)
        xf_lo = sb("xf_lo", [128, 2, 512], F16)
        gates = sb("gates", [128, 2, TILES, EXPERTS])
        hid = sb("hid", [128, 2, TOK])
        hid_hi = sb("hid_hi", [128, 4, TOK], F16)
        hid_lo = sb("hid_lo", [128, 4, TOK], F16)
        fs = sb("fs", [128, 2, 512])
        ts = sb("ts", [128, 512])
        bn_part = ts[:, 0:PAIRS * 6]
        xn = sb("xn", [128, TILES, D])
        xt_hi = sb("xt_hi", [128, TOK], F16)
        xt_lo = sb("xt_lo", [128, TOK], F16)
        ot_hi = (sb("ot_hi", [128, TOK], F16)[:], xt_hi[:])
        ot_lo = (sb("ot_lo", [128, TOK], F16)[:], xt_lo[:])
        qk_hi = sb("qk_hi", [128, 2, TOK], F16)
        qk_lo = sb("qk_lo", [128, 2, TOK], F16)
        q_sp = sb("q_sp", [128, GROUPS // 2 * TOK])
        k_sp = sb("k_sp", [128, GROUPS // 2 * TOK])
        v0 = sb("v0", [128, TILES, HEADS, HEAD + 1])
        minus_max = sb("minus_max", [128, TILES, GROUPS, 128], F16)
        pt = sb("pt", [128, 3, TOK])
        v1 = sb("v1", [128, TILES, HEADS, LIN_VALUE + 1])
        o1 = sb("o1", [128, TILES, HEADS, LIN_VALUE])
        st = sb("st", [128, TILES, 6])
        mv = sb("mv", [128, TILES, 2])
        ve = sb("ve", [128, TILES])
        rstd = sb("rstd", [128, TILES])
        rec = sb("rec", [128, 16])
        rec2 = sb("rec2", [128, 16])
        lg = sb("lg", [128, TILES, EXPERTS])
        lge = sb("lge", [128, TILES, EXPERTS])
        lmax = sb("lmax", [128, TILES])
        over = ts[:, 0:256].rearrange("p (t a b) -> p t a b", t=TILES, a=EXPERTS)
        same = ts[:, 256:512].rearrange("p (t a b) -> p t a b", t=TILES, a=EXPERTS)
        gate_t = fs[0:EXPERTS, 1, 0:TOK]
        row_max = sb("row_max", [128, 8])
        row_sum = sb("row_sum", [128, TILES, HEADS2])

        pa = ctx.enter_context(nc.psum_tensor("pa", [128, 4, 512], F32))
        pf = ctx.enter_context(nc.psum_tensor("pf", [128, 4, 512], F32))

        q16 = q_sp[:].bitcast(F16).rearrange("p (g t) -> p g t", g=GROUPS)
        k16 = k_sp[:].bitcast(F16).rearrange("p (g t) -> p g t", g=GROUPS)
        q2t, k2t = q_sp[:, 0:TOK], k_sp[:, 0:TOK]
        qkv = v1[:].rearrange("p t h d -> p (t h d)")[:, 0:TILES * 3 * D].rearrange("p (t c) -> p t c", t=TILES)
        squares = o1[:].rearrange("p t h d -> p (t h d)")[:, 0:TILES * 2 * D].rearrange("p (t c) -> p t c", t=TILES)
        o1_rows = o1[:].rearrange("p t h d -> p t (h d)")

        def W(name, first, width, rows_=128):
            c = COL[name] + first
            return w_hi[0:rows_, c:c + width], w_lo[0:rows_, c:c + width]

        def tile_cols(t):
            return slice(t * TILE, (t + 1) * TILE)

        started = sem("started")
        w_loaded = [sem(f"w_loaded{i}") for i in range(PIECES)]
        small_loaded = sem("small_loaded")
        const_done, consts_built = sem("const_done"), sem("consts_built")
        w_hi_done, w_lo_done = sem("w_hi_done"), sem("w_lo_done")
        derived = sem("derived")
        x_loaded = [sem("x_loaded0"), sem("x_loaded1")]
        x_turned, x_hi_done, x_lo_done = sem("x_turned"), sem("x_hi_done"), sem("x_lo_done")
        y_pre, y_ready, y_stats = sem("y_pre"), sem("y_ready"), sem("y_stats")
        bn_step = sem("bn_step")
        S = {}
        for name in ("z_ready z_turned h_ready ln_stats ln_aggr var_ready rstd_ready xn_ready turned hi_ready "
                     "lo_ready q_proj k_proj v_proj qk_hi_ready qk_lo_ready v_ready spread q_spread k_spread "
                     "s_raw s_max max_turned q_shifted st_ready p_exp p_band pv_done o_rec o_ready wo_ready "
                     "h_bo h_attn logit_ready l_biased l_max l_shifted l_exp l_sum l_rec probs ranks1 ranks2 "
                     "ranks3 ranks4 ranks5 gate_ready gate_turned gate_t_ready bias2_ready h_biased "
                     "el_exp el_min el_map qk_hi1 qk_lo1 v1_ones v1_proj v1_ready at_raw at_ready av_done den_done den_rec "
                     "o1_norm wo1_ready h_lin aff_ready qkv_proj qkv_ready sq_ready ss_sum ss_ready rn_ready "
                     "qkn_ready qk2_turned q2_ready k2_ready s2_raw s2_masked s2_max p2_ready p2_turned "
                     "p2t_ready pv2_done rs_rec o2_ready y_proj y_hi y_lo "
                     "pre_ready hid_ready hid_hi_done hid_lo_even hid_lo_odd hid_used gated").split():
            S[name] = sem(name)
        hid_lo_done = [S["hid_lo_even"], S["hid_lo_odd"]]
        out_sent = [sem("out_sent0"), sem("out_sent1")]

        block = ctx.enter_context(nc.Block())

        def half_of(kind, k, x):
            p = k * 2 + x
            before0, before1 = (p, k * 2) if kind == 0 else (k * 2 + 2, p)
            return before0 * 8 + before1 * 16

        def run_all(attention0, attention1, experts, n):
            def body(k, following):
                weave(experts(0, k, 0), attention0(k, 1), FFN_STEPS[0], A0_STEPS)
                weave(experts(0, k, 1), attention1(k, 0), FFN_STEPS[0], A1_STEPS)
                weave(experts(1, k, 0), attention1(k, 1), FFN_STEPS[1], A1_STEPS)
                if following:
                    weave(experts(1, k, 1), attention0(k + 1, 0), FFN_STEPS[1], A0_STEPS)
                else:
                    for _ in experts(1, k, 1):
                        pass

            for _ in attention0(0, 0):
                pass
            with n.loop(PAIRS // 2 - 1) as k:
                body(k, True)
            body(PAIRS // 2 - 1, False)

        @block.sync
        def _(sp):
            n = Counter(sp, "wait_sp")
            for i in range(PIECES):
                cols = slice(i * PIECE, (i + 1) * PIECE)
                sp.dma_start(y_all[:, cols], w_dram[:, cols]).then_inc(w_loaded[i], 16)
                if i == 0:
                    sp.dma_start(vec[:], vec_dram).then_inc(small_loaded, 16)
                    sp.dma_start(rows[:], row_dram.partition_broadcast(128)).then_inc(small_loaded, 16)
                    sp.dma_start(b2[:], b2_dram).then_inc(small_loaded, 16)
            sp.wait_ge(started, 1)
            with n.loop(PAIRS // 2) as k:
                for u in range(2):
                    sp.wait_ge(x_turned, n(k * 2 + u - 1))
                    src = x_dram[bass.ds(n.index(k * 4 + 2 * u), 2)].rearrange("b (w l) c -> l b w c", w=2)
                    dst = fs[:, u, 0:TILES * CHANNELS].rearrange("p (b w c) -> p b w c", b=2, w=2)
                    for b in range(2):
                        sp.dma_start(dst[:, b], src[:, b]).then_inc(x_loaded[u], 16)

            def store(k, x):
                before, _ = chunks_before(1, k, x)
                sp.wait_ge(S["gated"], n(before + EXPERTS))
                dst = out_dram[bass.ds(n.index(k * 4 + 2 * x), 2)].rearrange("b (t q) d -> q b t d", t=2)
                src = h[0:TILE, x].rearrange("p (b t) d -> p b t d", b=2)
                for b in range(2):
                    sp.dma_start(dst[:, b], src[:, b]).then_inc(out_sent[x], 16)

            with n.loop(PAIRS // 2) as k:
                store(k, 0)
                store(k, 1)
            for x in range(2):
                sp.wait_ge(out_sent[x], 32 * (PAIRS // 2))

        @block.gpsimd
        def _(pool):
            n = Counter(pool, "wait_pool")
            for s in S.values():
                pool.sem_inc(s, START)
            for s in (x_turned, x_hi_done, x_lo_done, y_pre, y_ready, y_stats):
                pool.sem_inc(s, START)
            pool.sem_inc(started, 1)
            steps = [0]

            def const(instruction):
                instruction.then_inc(const_done, 1)
                steps[0] += 1
                pool.wait_ge(const_done, steps[0])

            def keep(view, base, pattern, channel, fill, compare=ALU.is_ge):
                const(nc.gpsimd.affine_select(out=view, in_=view, compare_op=compare, fill=fill, base=base,
                                              pattern=pattern, channel_multiplier=channel))

            for view, value in ((ident[:], 0.0), (ident16[:], 0.0), (pick_q_hi[:], 0.0), (pick_q_lo[:], 0.0),
                                (pick_k_hi[:], 0.0), (pick_k_lo[:], 0.0), (one_row[:], 0.0),
                                (band[:], float(np.exp(np.float32(0.1)))), (causal[:], 1.0), (causal_add[:], 0.0),
                                (earlier[:], 1.0), (minus_half[:], -0.5), (v0[:], 1.0), (minus_max[:], 0.0)):
                const(nc.gpsimd.memset(view, value))
            keep(ident[:], 0, [[-1, 128]], 1, 1.0, ALU.not_equal)
            keep(ident16[:], 0, [[-1, 128]], 1, 1.0, ALU.not_equal)
            for matrix, copies in ((pick_q_hi, (0, 1)), (pick_q_lo, (2,)), (pick_k_hi, (0, 2)), (pick_k_lo, (1,))):
                for g in range(GROUPS):
                    for r in copies:
                        view = matrix[:, g, :].rearrange("p (j r d) -> p j r d", j=2, d=HEAD)[:, :, r, :]
                        keep(view, -32 * g, [[-HEAD, 2], [-1, HEAD]], 1, 1.0, ALU.not_equal)
            keep(one_row[:], -48, [[0, 1]], 1, 1.0, ALU.not_equal)
            keep(one_row[:], -112, [[0, 1]], 1, 1.0, ALU.not_equal)
            keep(band[:], BAND, [[-5, 2], [1, BAND_WIDTH]], -1, 1.0)
            keep(band[:], BAND, [[5, 2], [-1, BAND_WIDTH]], 1, 1.0)
            for t in (0, 2):
                keep(causal[:, t, :], 0, [[1, TILE]], -1, 0.0)
                keep(causal_add[:, t, :], 0, [[-1, TILE]], 1, -1e30)
            keep(earlier[:], -1, [[1, EXPERTS], [-1, EXPERTS]], 0, 0.0)
            pool.sem_inc(consts_built, 1)
            pool.wait_ge(bn_step, 2)
            nc.gpsimd.tensor_tensor(bn_rstd[:], bn_var[:], minus_half[:, 0:1], ALU.pow).then_inc(bn_step, 1)

            def norm(f2):
                pool.wait_ge(S["var_ready"], n(f2 + 1))
                nc.gpsimd.tensor_tensor(rstd[0:TILE], ve[0:TILE], minus_half[0:TILE, 0:TILES],
                                        ALU.pow).then_inc(S["rstd_ready"], 1)

            def softmax_attention(k, x):
                p, f, _ = phase_of("A0", k, x)
                yield
                norm(f * 2)
                yield
                for _ in range(4):
                    yield
                pool.wait_ge(S["xn_ready"], n(f * 2 + 1))
                bo = rows[0:TILE, R_BO:R_BO + D].unsqueeze(1).to_broadcast([TILE, TILES, D])
                nc.gpsimd.tensor_tensor(h[0:TILE, x], h[0:TILE, x], bo, ALU.add).then_inc(S["h_bo"], 1)
                for _ in range(5):
                    yield
                for i in range(16):
                    if i and i % 4 == 0:
                        yield
                    pool.wait_ge(S["p_exp"], n(p * 16 + i + 1))
                    strip = pt[0:TILE, i % 3, :].copy()
                    strip = bass.AP(strip.tensor, strip.offset, [list(strip.ap[0]), [SEQ + TILE - BAND, 2],
                                                                 [1, BAND_WIDTH]])
                    nc.gpsimd.tensor_tensor(strip, strip, band[0:TILE], ALU.mult).then_inc(S["p_band"], 1)
                for _ in range(4):
                    yield
                norm(f * 2 + 1)
                for _ in range(5):
                    yield

            def linear_and_causal_attention(k, x):
                p, f, _ = phase_of("A1", k, x)
                norm(f * 2)
                yield
                yield
                counted = n(f)
                pool.wait_ge(started, 1)
                pool.wait_ge(S["h_biased"], counted)
                nc.gpsimd.memset(v1[0:TILE, :, :, LIN_VALUE:LIN_VALUE + 1], 1.0).then_inc(S["v1_ones"], 1)
                for _ in range(13):
                    yield
                norm(f * 2 + 1)
                for _ in range(3):
                    yield
                pool.wait_ge(S["qkv_ready"], n(p * 4 + 4))
                nc.gpsimd.tensor_tensor(squares[0:TILE], qkv[0:TILE, :, 0:2 * D], qkv[0:TILE, :, 0:2 * D],
                                        ALU.mult).then_inc(S["sq_ready"], 1)
                pool.wait_ge(S["ss_ready"], n(p + 1))
                nc.gpsimd.tensor_tensor(rec2[0:TILE], rec[0:TILE], minus_half[0:TILE, 0:16],
                                        ALU.pow).then_inc(S["rn_ready"], 1)
                for _ in range(13):
                    yield

            def experts(kind, k, x):
                _, before = chunks_before(kind, k, x)
                total = EXPERTS * (CHUNKS0, CHUNKS1)[kind]
                for c in range(total + LAG):
                    if c < total and c % 2 == 1:
                        pool.wait_ge(S["hid_hi_done"], n(before + c + 1))
                        nc.gpsimd.tensor_tensor(hid_lo[:, c % 4], hid[:, 1], hid_hi[:, c % 4],
                                                ALU.subtract).then_inc(hid_lo_done[1], 1)
                    yield

            run_all(softmax_attention, linear_and_causal_attention, experts, n)

        @block.scalar
        def _(act):
            n = Counter(act, "wait_act")
            act.wait_ge(started, 1)
            for i in range(PIECES):
                cols = slice(i * PIECE, (i + 1) * PIECE)
                act.wait_ge(w_loaded[i], 16)
                nc.scalar.copy(w_hi[:, cols], y_all[:, cols]).then_inc(w_hi_done, 1)

            def tokenize(k, u):
                p = k * 2 + u
                act.wait_ge(x_turned, n(p + 1))
                act.wait_ge(y_pre, n(p - 1))
                nc.scalar.copy(xf_hi[0:CHANNELS, u], pf[0:CHANNELS, u]).then_inc(x_hi_done, 1)

            def relu(k, u):
                p = k * 2 + u
                act.wait_ge(y_pre, n(p + 1))
                nc.scalar.activation(y_all[:, bass.ds(n.index(p * TOK), TOK)], pf[:, 2 + u, 0:TOK], ACT.Relu,
                                     bias=vec[:, V_TOKB:V_TOKB + 1]).then_inc(y_ready, 1)

            act.wait_ge(small_loaded, 48)
            act.wait_ge(w_lo_done, PIECES)
            tokenize(0, 0)
            with n.loop(PAIRS // 2 - 1) as k:
                tokenize(k, 1)
                relu(k, 0)
                tokenize(k + 1, 0)
                relu(k, 1)
            tokenize(PAIRS // 2 - 1, 1)
            relu(PAIRS // 2 - 1, 0)
            relu(PAIRS // 2 - 1, 1)

            def high(t, dst, bank=1, scale=1.0, bias=0.0):
                act.wait_ge(S["turned"], n(t + 1))
                nc.scalar.activation(dst, pa[:, bank, 0:TOK], ACT.Identity, scale=scale,
                                     bias=bias).then_inc(S["hi_ready"], 1)

            def spread_keys(f):
                for g in range(GROUPS):
                    act.wait_ge(S["spread"], n(f * 8 + GROUPS + g + 1))
                    nc.scalar.activation(k16[:, g], pa[:, g, 0:TOK], ACT.Identity,
                                         bias=one_row[:, 0:1]).then_inc(S["k_spread"], 1)

            def gate(f):
                act.wait_ge(S["l_shifted"], n(f + 1))
                nc.scalar.activation(lge[0:TILE], lg[0:TILE], ACT.Exp).then_inc(S["l_exp"], 1)
                yield
                act.wait_ge(S["gate_turned"], n(f + 1))
                nc.scalar.copy(gate_t, pa[0:EXPERTS, 3, 0:TOK]).then_inc(S["gate_t_ready"], 1)
                yield
                yield

            def softmax_attention(k, x):
                p, f, t = phase_of("A0", k, x)
                yield
                act.wait_ge(S["z_turned"], n(p + 1))
                act.wait_ge(out_sent[x], n.plain(k * 32))
                nc.scalar.copy(h[0:TILE, x], pa[0:TILE, 0].rearrange("p (t d) -> p t d", t=TILES)
                               ).then_inc(S["h_ready"], 1)
                yield
                high(t, xt_hi[:])
                yield
                act.wait_ge(S["q_proj"], n(f + 1))
                nc.scalar.activation(qk_hi[:, 0], pa[:, 0, 0:TOK], ACT.Identity,
                                     bias=q_bias[:, 0:1]).then_inc(S["qk_hi_ready"], 1)
                act.wait_ge(S["k_proj"], n(f + 1))
                nc.scalar.activation(qk_hi[:, 1], pa[:, 2, 0:TOK], ACT.Identity,
                                     bias=vec[:, V_BK:V_BK + 1]).then_inc(S["qk_hi_ready"], 1)
                yield
                yield
                spread_keys(f)
                yield
                for _ in range(5):
                    yield
                for i in range(16):
                    if i and i % 4 == 0:
                        yield
                    act.wait_ge(S["st_ready"], n(p * 16 + i + 1))
                    act.wait_ge(S["pv_done"], n(p * 16 + i - 2))
                    nc.scalar.activation(pt[0:TILE, i % 3], pa[0:TILE, i % 2, 0:TOK], ACT.Exp,
                                         scale=HEAD ** -0.5).then_inc(S["p_exp"], 1)
                yield
                yield
                high(t + 1, ot_hi[0])
                yield
                yield
                yield
                high(t + 2, xf_hi[:, x, 0:TOK])
                yield
                yield from gate(f)

            def linear_and_causal_attention(k, x):
                p, f, t = phase_of("A1", k, x)
                yield
                high(t, xt_hi[:])
                yield
                act.wait_ge(S["q_proj"], n(f + 1))
                nc.scalar.activation(fs[:, 0, 0:TOK], pa[:, 0, 0:TOK], ACT.Exp).then_inc(S["el_exp"], 1)
                act.wait_ge(S["k_proj"], n(f + 1))
                nc.scalar.activation(fs[:, 1, 0:TOK], pa[:, 2, 0:TOK], ACT.Exp).then_inc(S["el_exp"], 1)
                yield
                act.wait_ge(S["v1_ones"], n(p + 1))
                for i in range(TILES):
                    act.wait_ge(S["v1_proj"], n(p * 4 + i + 1))
                    nc.scalar.copy(v1[0:TILE, i, :, 0:LIN_VALUE],
                                   pa[0:TILE, (3, 1)[i % 2]].rearrange("p (h d) -> p h d", h=HEADS)
                                   ).then_inc(S["v1_ready"], 1)
                yield
                yield
                spread_keys(f)
                yield
                for _ in range(5):
                    yield
                for c in range(4):
                    high(t + 1 + c, ot_hi[c % 2])
                    yield
                yield
                high(t + 5, xt_hi[:], 1, vec[:, V_LNG:V_LNG + 1], vec[:, V_LNB:V_LNB + 1])
                yield
                for i in range(TILES):
                    act.wait_ge(S["qkv_proj"], n(p * 4 + i + 1))
                    nc.scalar.copy(qkv[0:TILE, i], pa[0:TILE, (0, 2, 3, 1)[i], 0:3 * D]
                                   ).then_inc(S["qkv_ready"], 1)
                yield
                yield
                act.wait_ge(S["qk2_turned"], n(p * 2 + 2))
                nc.scalar.copy(k2t, pa[:, 2, 0:TOK]).then_inc(S["k2_ready"], 1)
                yield
                for i in range(6):
                    if i < 4:
                        act.wait_ge(S["s2_max"], n(p * 4 + i + 1))
                        b, hd = i // 2, i % 2
                        for qt, cols in ((0, slice(0, TILE)), (1, slice(TILE, 3 * TILE))):
                            last = nc.scalar.activation(pt[0:TILE, i % 2, cols], pt[0:TILE, i % 2, cols], ACT.Exp,
                                                        bias=row_max[0:TILE, 2 * i + qt:2 * i + qt + 1],
                                                        accum_out=row_sum[0:TILE, 2 * b + qt, hd:hd + 1])
                        last.then_inc(S["p2_ready"], 1)
                    if 1 <= i <= 4:
                        act.wait_ge(S["p2_turned"], n(p * 4 + i))
                        act.wait_ge(S["pv2_done"], n(p * 4 + i - 2))
                        nc.scalar.copy(fs[0:TILE, (i - 1) % 2, 0:3 * TILE],
                                       pa[0:TILE, 1, 0:3 * TILE]).then_inc(S["p2t_ready"], 1)
                    yield
                high(t + 6, ot_hi[0])
                yield
                act.wait_ge(S["y_proj"], n(p + 1))
                nc.scalar.copy(xf_hi[:, x, 0:TOK], pa[:, 0, 0:TOK]).then_inc(S["y_hi"], 1)
                yield
                yield from gate(f)

            def experts(kind, k, x):
                _, before = chunks_before(kind, k, x)
                per = (CHUNKS0, CHUNKS1)[kind]
                bias0 = (V_B0, V_B1)[kind]
                func = (ACT.Gelu, ACT.Gelu_apprx_tanh)[kind]
                half = half_of(kind, k, x)
                for c in range(EXPERTS * per + LAG):
                    if c < EXPERTS * per:
                        act.wait_ge(S["pre_ready"], n(before + c + 1))
                        act.wait_ge(hid_lo_done[c % 2], n(half + c // 2))
                        nc.scalar.activation(hid[:, c % 2], pf[:, c % 2, 0:TOK], func,
                                             bias=vec[:, bias0 + c:bias0 + c + 1]).then_inc(S["hid_ready"], 1)
                    yield

            run_all(softmax_attention, linear_and_causal_attention, experts, n)

        @block.vector
        def _(dve):
            n = Counter(dve, "wait_dve")
            dve.wait_ge(started, 1)
            for i in range(PIECES):
                cols = slice(i * PIECE, (i + 1) * PIECE)
                dve.wait_ge(w_hi_done, i + 1)
                nc.vector.tensor_tensor(w_lo[:, cols], y_all[:, cols], w_hi[:, cols],
                                        ALU.subtract).then_inc(w_lo_done, 1)
            dve.wait_ge(small_loaded, 48)
            nc.vector.tensor_tensor(q_bias[:], vec[:, V_BQ:V_BQ + 1], vec[:, V_OCR:V_OCR + 1],
                                    ALU.add).then_inc(derived, 1)
            nc.vector.scalar_tensor_tensor(qk_gain[:], vec[:, V_QN:V_QN + 1], float(HEAD2) ** 0.5,
                                           vec[:, V_KN:V_KN + 1], ALU.mult, ALU.mult).then_inc(derived, 1)
            dve.wait_ge(derived, 2)

            def low(k, u):
                p = k * 2 + u
                dve.wait_ge(x_hi_done, n(p + 1))
                nc.vector.tensor_tensor(xf_lo[0:CHANNELS, u], pf[0:CHANNELS, u], xf_hi[0:CHANNELS, u],
                                        ALU.subtract).then_inc(x_lo_done, 1)

            def stats(k, u):
                p = k * 2 + u
                dve.wait_ge(y_ready, n(p + 1))
                nc.vector.bn_stats(bn_part[:, bass.ds(n.index(p * 6), 6)],
                                   y_all[:, bass.ds(n.index(p * TOK), TOK)]).then_inc(y_stats, 1)

            low(0, 0)
            with n.loop(PAIRS // 2 - 1) as k:
                low(k, 1)
                stats(k, 0)
                low(k + 1, 0)
                stats(k, 1)
            low(PAIRS // 2 - 1, 1)
            stats(PAIRS // 2 - 1, 0)
            stats(PAIRS // 2 - 1, 1)
            dve.wait_ge(y_stats, n(PAIRS))
            nc.vector.bn_aggr(bn[:], bn_part).then_inc(bn_step, 1)
            dve.wait_ge(bn_step, 1)
            nc.vector.tensor_scalar(bn_var[:], bn[:, 1:2], EPS, None, ALU.add).then_inc(bn_step, 1)
            dve.wait_ge(bn_step, 3)
            nc.vector.tensor_tensor(bn_scale[:], bn_rstd[:], vec[:, V_GAMMA:V_GAMMA + 1], ALU.mult
                                    ).then_inc(bn_step, 1)
            dve.wait_ge(bn_step, 4)
            nc.vector.scalar_tensor_tensor(bn_shift[:], bn[:, 0:1], bn_scale[:, 0:1], vec[:, V_BETA:V_BETA + 1],
                                           ALU.mult, ALU.subtract).then_inc(bn_step, 1)
            dve.wait_ge(bn_step, 5)

            def norm_stats(f2, x, twice=False):
                for i in range(TILES):
                    last = nc.vector.bn_stats(st[0:TILE, i], h[0:TILE, x, i])
                last.then_inc(S["ln_stats"], 1)
                counted = n(f2 + 1)
                dve.wait_ge(started, 1)
                dve.wait_ge(S["ln_stats"], counted)
                for i in range(TILES):
                    last = nc.vector.bn_aggr(mv[0:TILE, i], st[0:TILE, i])
                last.then_inc(S["ln_aggr"], 1)
                dve.wait_ge(S["ln_aggr"], n(f2 + 1))
                scale, shift = (1.0 + EPS, EPS * EPS) if twice else (1.0, EPS)
                nc.vector.tensor_scalar(ve[0:TILE], mv[0:TILE, :, 1], scale, shift, ALU.mult,
                                        ALU.add).then_inc(S["var_ready"], 1)

            def norm_apply(f2, x, t):
                dve.wait_ge(S["rstd_ready"], n(f2 + 1))
                dve.wait_ge(S["turned"], n(t))
                for i in range(TILES):
                    last = nc.vector.tensor_scalar(xn[0:TILE, i], h[0:TILE, x, i], mv[0:TILE, i, 0:1],
                                                   rstd[0:TILE, i:i + 1], ALU.subtract, ALU.mult)
                last.then_inc(S["xn_ready"], 1)

            def low_part(t, dst, hi):
                dve.wait_ge(S["hi_ready"], n(t + 1))
                nc.vector.tensor_tensor(dst, pa[:, 1, 0:TOK], hi, ALU.subtract).then_inc(S["lo_ready"], 1)

            def spread_queries(f):
                for g in range(GROUPS):
                    dve.wait_ge(S["spread"], n(f * 8 + g + 1))
                    nc.vector.tensor_copy(q16[:, g], pa[:, g, 0:TOK]).then_inc(S["q_spread"], 1)

            def wide(ap):
                return ap.unsqueeze(2).to_broadcast([TILE, TILES, EXPERTS])

            def gate(p, f, x, kind):
                dve.wait_ge(S["logit_ready"], n(f + 1))
                first = (R_G0, R_G1)[kind]
                bias = rows[0:TILE, first:first + EXPERTS].unsqueeze(1).to_broadcast([TILE, TILES, EXPERTS])
                logits = pa[0:TILE, 2, 0:TILES * EXPERTS].rearrange("p (t e) -> p t e", t=TILES)
                nc.vector.tensor_tensor(lg[0:TILE], logits, bias, ALU.add).then_inc(S["l_biased"], 1)
                dve.wait_ge(S["l_biased"], n(f + 1))
                nc.vector.tensor_reduce(lmax[0:TILE], lg[0:TILE], AX.X, ALU.max).then_inc(S["l_max"], 1)
                dve.wait_ge(S["l_max"], n(f + 1))
                nc.vector.tensor_tensor(lg[0:TILE], lg[0:TILE], wide(lmax[0:TILE]),
                                        ALU.subtract).then_inc(S["l_shifted"], 1)
                yield
                dve.wait_ge(S["l_exp"], n(f + 1))
                nc.vector.tensor_reduce(ve[0:TILE], lge[0:TILE], AX.X, ALU.add).then_inc(S["l_sum"], 1)
                dve.wait_ge(S["l_sum"], n(f + 1))
                nc.vector.reciprocal(lmax[0:TILE], ve[0:TILE]).then_inc(S["l_rec"], 1)
                dve.wait_ge(S["l_rec"], n(f + 1))
                if kind == 1:
                    nc.vector.tensor_tensor(gates[0:TILE, x], lge[0:TILE], wide(lmax[0:TILE]),
                                            ALU.mult).then_inc(S["gate_ready"], 1)
                else:
                    nc.vector.tensor_tensor(lg[0:TILE], lge[0:TILE], wide(lmax[0:TILE]),
                                            ALU.mult).then_inc(S["probs"], 1)
                    dve.wait_ge(S["probs"], n(p + 1))
                    mine = lg[0:TILE].unsqueeze(3).to_broadcast([TILE, TILES, EXPERTS, EXPERTS])
                    other = lg[0:TILE].unsqueeze(2).to_broadcast([TILE, TILES, EXPERTS, EXPERTS])
                    nc.vector.tensor_tensor(over[0:TILE], other, mine, ALU.is_gt).then_inc(S["ranks1"], 1)
                    nc.vector.tensor_tensor(same[0:TILE], other, mine, ALU.is_equal).then_inc(S["ranks2"], 1)
                    dve.wait_ge(S["ranks2"], n(p + 1))
                    flat = earlier[0:TILE].rearrange("p a b -> p (a b)").unsqueeze(1).to_broadcast(
                        [TILE, TILES, EXPERTS * EXPERTS])
                    same_flat = same[0:TILE].rearrange("p t a b -> p t (a b)")
                    nc.vector.tensor_tensor(same_flat, same_flat, flat, ALU.mult).then_inc(S["ranks3"], 1)
                    dve.wait_ge(S["ranks3"], n(p + 1))
                    nc.vector.tensor_tensor(over[0:TILE], over[0:TILE], same[0:TILE],
                                            ALU.add).then_inc(S["ranks4"], 1)
                    dve.wait_ge(S["ranks4"], n(p + 1))
                    nc.vector.tensor_reduce(lge[0:TILE], over[0:TILE], AX.X, ALU.add).then_inc(S["ranks5"], 1)
                    dve.wait_ge(S["ranks5"], n(p + 1))
                    nc.vector.scalar_tensor_tensor(gates[0:TILE, x], lge[0:TILE], 2.0, lg[0:TILE], ALU.is_lt,
                                                   ALU.mult).then_inc(S["gate_ready"], 1)
                yield
                dve.wait_ge(S["bias2_ready"], n(f + 1))
                nc.vector.tensor_tensor(h[0:TILE, x], pa[0:TILE, 0].rearrange("p (t d) -> p t d", t=TILES),
                                        h[0:TILE, x], ALU.add).then_inc(S["h_biased"], 1)
                yield

            def softmax_attention(k, x):
                p, f, t = phase_of("A0", k, x)
                dve.wait_ge(S["z_turned"], n(p))
                nc.vector.tensor_scalar(fs[:, 0, 0:TOK], y_all[:, bass.ds(n.index(p * TOK), TOK)], bn_scale[:, 0:1],
                                        bn_shift[:, 0:1], ALU.mult, ALU.subtract).then_inc(S["z_ready"], 1)
                yield
                dve.wait_ge(S["h_ready"], n(p + 1))
                norm_stats(f * 2, x)
                yield
                norm_apply(f * 2, x, t)
                low_part(t, xt_lo[:], xt_hi[:])
                yield
                dve.wait_ge(S["qk_hi_ready"], n(p * 2 + 1))
                nc.vector.scalar_tensor_tensor(qk_lo[:, 0], pa[:, 0, 0:TOK], q_bias[:, 0:1], qk_hi[:, 0], ALU.add,
                                               ALU.subtract).then_inc(S["qk_lo_ready"], 1)
                dve.wait_ge(S["qk_hi_ready"], n(p * 2 + 2))
                nc.vector.scalar_tensor_tensor(qk_lo[:, 1], pa[:, 2, 0:TOK], vec[:, V_BK:V_BK + 1], qk_hi[:, 1],
                                               ALU.add, ALU.subtract).then_inc(S["qk_lo_ready"], 1)
                dve.wait_ge(S["v_proj"], n(p + 1))
                bv = rows[0:TILE, R_BV:R_BV + D].rearrange("p (h d) -> p h d", h=HEADS)
                for i in range(TILES):
                    last = nc.vector.tensor_tensor(v0[0:TILE, i, :, 0:HEAD],
                                                   pa[0:TILE, 3, i * D:(i + 1) * D].rearrange(
                                                       "p (h d) -> p h d", h=HEADS), bv, ALU.add)
                last.then_inc(S["v_ready"], 1)
                yield
                spread_queries(f)
                yield
                yield
                for i in range(16):
                    if i and i % 4 == 0:
                        yield
                    b, hd = i // HEADS, i % HEADS
                    dve.wait_ge(S["s_raw"], n(p * 16 + i + 1))
                    col = 64 * (hd % 2) + 48
                    nc.vector.tensor_reduce(minus_max[0:TILE, 2 * b:2 * b + 2, hd // 2, col],
                                            pa[0:TILE, i % 2, 0:TOK].rearrange("p (t k) -> p t k", t=2),
                                            AX.X, ALU.max, negate=True).then_inc(S["s_max"], 1)
                yield
                for g in range(GROUPS):
                    dve.wait_ge(S["max_turned"], n(p * 4 + g + 1))
                    nc.vector.tensor_tensor(q16[:, g], pa[:, 2 + g % 2, 0:TOK], q16[:, g],
                                            ALU.add).then_inc(S["q_shifted"], 1)
                yield
                yield
                yield

                def divide(b):
                    dve.wait_ge(S["pv_done"], n(p * 16 + 8 * b + 8))
                    dve.wait_ge(S["o_ready"], n(p * 2 + b))
                    o = pa[0:TILE, 2 + b, 0:2 * HEADS * (HEAD + 1)].rearrange("p (t d) -> p t d", d=HEAD + 1)
                    nc.vector.reciprocal(rec[0:TILE], o[:, :, HEAD]).then_inc(S["o_rec"], 1)
                    dve.wait_ge(S["o_rec"], n(p * 2 + b + 1))
                    nc.vector.tensor_tensor(
                        xn[0:TILE, 2 * b:2 * b + 2].rearrange("p t (h d) -> p (t h) d", d=HEAD), o[:, :, 0:HEAD],
                        rec[0:TILE].unsqueeze(2).to_broadcast([TILE, 16, HEAD]), ALU.mult
                    ).then_inc(S["o_ready"], 1)

                yield
                divide(0)
                yield
                divide(1)
                yield
                low_part(t + 1, ot_lo[0], ot_hi[0])
                yield
                dve.wait_ge(S["wo_ready"], n(p + 1))
                dve.wait_ge(S["h_bo"], n(p + 1))
                nc.vector.tensor_tensor(h[0:TILE, x], pa[0:TILE, 0].rearrange("p (t d) -> p t d", t=TILES),
                                        h[0:TILE, x], ALU.add).then_inc(S["h_attn"], 1)
                dve.wait_ge(S["h_attn"], n(p + 1))
                norm_stats(f * 2 + 1, x)
                yield
                norm_apply(f * 2 + 1, x, t + 2)
                yield
                low_part(t + 2, xf_lo[:, x, 0:TOK], xf_hi[:, x, 0:TOK])
                yield
                yield from gate(p, f, x, 0)

            def linear_and_causal_attention(k, x):
                p, f, t = phase_of("A1", k, x)
                before, _ = chunks_before(0, k, x)
                dve.wait_ge(S["gated"], n(before + EXPERTS))
                norm_stats(f * 2, x)
                yield
                norm_apply(f * 2, x, t)
                low_part(t, xt_lo[:], xt_hi[:])
                yield
                for j, bank in ((0, 0), (1, 2)):
                    c = p * 2 + j + 1
                    dve.wait_ge(S["el_exp"], n(c))
                    nc.vector.tensor_scalar(ts[:, 0:TOK], fs[:, j, 0:TOK], 1.0, None, ALU.min).then_inc(S["el_min"], 1)
                    dve.wait_ge(S["el_min"], n(c))
                    nc.vector.scalar_tensor_tensor(fs[:, j, 0:TOK], pa[:, bank, 0:TOK], 0.0, ts[:, 0:TOK], ALU.max,
                                                   ALU.add).then_inc(S["el_map"], 1)
                    dve.wait_ge(S["el_map"], n(c))
                    nc.vector.tensor_copy(qk_hi[:, j], fs[:, j, 0:TOK]).then_inc(S["qk_hi1"], 1)
                    dve.wait_ge(S["qk_hi1"], n(c))
                    nc.vector.tensor_tensor(qk_lo[:, j], fs[:, j, 0:TOK], qk_hi[:, j],
                                            ALU.subtract).then_inc(S["qk_lo1"], 1)
                yield
                yield
                spread_queries(f)
                yield
                yield

                def divide(g8):
                    b, g = g8 // 4, g8 % 4
                    dve.wait_ge(S["av_done"], n(p * 16 + 2 * g8 + 2))
                    bank = pa[0:TILE, 2 + g8 % 2, 0:4 * (LIN_VALUE + 1)].rearrange(
                        "p (h t d) -> p h t d", h=2, t=2)
                    den = rec[0:TILE, 0:4].rearrange("p (h t) -> p h t", h=2)
                    nc.vector.tensor_scalar(den, bank[:, :, :, LIN_VALUE], 1e-6, None, ALU.max
                                            ).then_inc(S["den_done"], 1)
                    dve.wait_ge(S["den_done"], n(p * 8 + g8 + 1))
                    nc.vector.reciprocal(rec2[0:TILE, 0:4], rec[0:TILE, 0:4]).then_inc(S["den_rec"], 1)
                    dve.wait_ge(S["den_rec"], n(p * 8 + g8 + 1))
                    inv = rec2[0:TILE, 0:4].rearrange("p (h t) -> p h t", h=2).unsqueeze(3).to_broadcast(
                        [TILE, 2, 2, LIN_VALUE])
                    dst = o1[0:TILE, 2 * b:2 * b + 2, 2 * g:2 * g + 2, :].rearrange("p t h d -> p h t d")
                    nc.vector.tensor_tensor(dst, bank[:, :, :, 0:LIN_VALUE], inv, ALU.mult
                                            ).then_inc(S["o1_norm"], 1)

                for i in range(18):
                    if i and i % 4 == 0:
                        yield
                    if i < 16:
                        dve.wait_ge(S["at_raw"], n(p * 16 + i + 1))
                        dve.wait_ge(S["av_done"], n(p * 16 + i - 2))
                        nc.vector.tensor_tensor(pt[0:TILE, i % 3, 0:3 * TILE], pa[0:TILE, i % 2, 0:3 * TILE],
                                                causal[0:TILE].rearrange("p a b -> p (a b)"),
                                                ALU.mult).then_inc(S["at_ready"], 1)
                    if i >= 3 and i % 2 == 1:
                        divide((i - 3) // 2)
                yield
                for c in range(4):
                    low_part(t + 1 + c, ot_lo[c % 2], ot_hi[c % 2])
                    yield
                dve.wait_ge(S["wo1_ready"], n(p + 1))
                nc.vector.tensor_tensor(h[0:TILE, x], pa[0:TILE, 0].rearrange("p (t d) -> p t d", t=TILES),
                                        h[0:TILE, x], ALU.add).then_inc(S["h_lin"], 1)
                dve.wait_ge(S["h_lin"], n(p + 1))
                norm_stats(f * 2 + 1, x, True)
                yield
                norm_apply(f * 2 + 1, x, t + 5)
                dve.wait_ge(S["hi_ready"], n(t + 6))
                nc.vector.tensor_scalar(fs[:, 0, 0:TOK], pa[:, 1, 0:TOK], vec[:, V_LNG:V_LNG + 1],
                                        vec[:, V_LNB:V_LNB + 1], ALU.mult, ALU.add).then_inc(S["aff_ready"], 1)
                dve.wait_ge(S["aff_ready"], n(p + 1))
                nc.vector.tensor_tensor(xt_lo[:], fs[:, 0, 0:TOK], xt_hi[:], ALU.subtract).then_inc(S["lo_ready"], 1)
                yield
                yield
                dve.wait_ge(S["sq_ready"], n(p + 1))
                nc.vector.tensor_reduce(rec2[0:TILE].rearrange("p (t c) -> p t c", t=TILES),
                                        squares[0:TILE].rearrange("p t (c d) -> p t c d", d=HEAD2), AX.X,
                                        ALU.add).then_inc(S["ss_sum"], 1)
                dve.wait_ge(S["ss_sum"], n(p + 1))
                nc.vector.tensor_scalar(rec[0:TILE], rec2[0:TILE], 1e-12, None, ALU.add).then_inc(S["ss_ready"], 1)
                dve.wait_ge(S["rn_ready"], n(p + 1))
                heads = qkv[0:TILE, :, 0:2 * D].rearrange("p t (c d) -> p t c d", d=HEAD2)
                inv = rec2[0:TILE].rearrange("p (t c) -> p t c", t=TILES).unsqueeze(3).to_broadcast(
                    [TILE, TILES, 4, HEAD2])
                nc.vector.tensor_tensor(heads, heads, inv, ALU.mult).then_inc(S["qkn_ready"], 1)
                yield
                dve.wait_ge(S["qk2_turned"], n(p * 2 + 1))
                nc.vector.tensor_scalar(q2t, pa[:, 0, 0:TOK], qk_gain[:, 0:1], None, ALU.mult
                                        ).then_inc(S["q2_ready"], 1)
                yield
                for i in range(6):
                    if i < 4:
                        dve.wait_ge(S["s2_raw"], n(p * 4 + i + 1))
                        dve.wait_ge(S["p2_turned"], n(p * 4 + i - 1))
                        nc.vector.tensor_tensor(pt[0:TILE, i % 2, 0:3 * TILE], pa[0:TILE, 2 * (i % 2), 0:3 * TILE],
                                                causal_add[0:TILE].rearrange("p a b -> p (a b)"),
                                                ALU.add).then_inc(S["s2_masked"], 1)
                        dve.wait_ge(S["s2_masked"], n(p * 4 + i + 1))
                        for qt, cols in ((0, slice(0, TILE)), (1, slice(TILE, 3 * TILE))):
                            last = nc.vector.tensor_reduce(row_max[0:TILE, 2 * i + qt:2 * i + qt + 1],
                                                           pt[0:TILE, i % 2, cols], AX.X, ALU.max, negate=True)
                        last.then_inc(S["s2_max"], 1)
                    if i < 5:
                        yield
                dve.wait_ge(S["pv2_done"], n(p * 4 + 4))
                nc.vector.reciprocal(rec[0:TILE, 0:8], row_sum[0:TILE].rearrange("p t h -> p (t h)")
                                     ).then_inc(S["rs_rec"], 1)
                dve.wait_ge(S["rs_rec"], n(p + 1))
                nc.vector.tensor_tensor(
                    xn[0:TILE].rearrange("p t (h d) -> p (t h) d", d=HEAD2),
                    pa[0:TILE, 3].rearrange("p (c d) -> p c d", d=HEAD2),
                    rec[0:TILE, 0:8].unsqueeze(2).to_broadcast([TILE, 8, HEAD2]), ALU.mult
                ).then_inc(S["o2_ready"], 1)
                yield
                low_part(t + 6, ot_lo[0], ot_hi[0])
                yield
                dve.wait_ge(S["y_hi"], n(p + 1))
                nc.vector.tensor_tensor(xf_lo[:, x, 0:TOK], pa[:, 0, 0:TOK], xf_hi[:, x, 0:TOK],
                                        ALU.subtract).then_inc(S["y_lo"], 1)
                yield
                yield from gate(p, f, x, 1)

            def experts(kind, k, x):
                experts_before, before = chunks_before(kind, k, x)
                half = half_of(kind, k, x)
                _, f, _ = phase_of(("A0", "A1")[kind], k, x)
                per = (CHUNKS0, CHUNKS1)[kind]
                total = EXPERTS * per
                for c in range(total + LAG):
                    if c < total:
                        dve.wait_ge(S["hid_ready"], n(before + c + 1))
                        dve.wait_ge(S["hid_used"], n(before + c - 3))
                        nc.vector.tensor_copy(hid_hi[:, c % 4], hid[:, c % 2]).then_inc(S["hid_hi_done"], 1)
                        if c % 2 == 0:
                            dve.wait_ge(S["hid_hi_done"], n(before + c + 1))
                            nc.vector.tensor_tensor(hid_lo[:, c % 4], hid[:, 0], hid_hi[:, c % 4],
                                                    ALU.subtract).then_inc(hid_lo_done[0], 1)
                    if c >= LAG and (c - LAG) % per == per - 1:
                        e = (c - LAG) // per
                        dve.wait_ge(S["hid_used"], n(before + (e + 1) * per))
                        if e == 0:
                            dve.wait_ge(S["h_biased"], n(f + 1))
                        dve.wait_ge(S["gated"], n(experts_before + e))
                        for i in range(TILES):
                            last = nc.vector.scalar_tensor_tensor(
                                h[0:TILE, x, i], pf[0:TILE, 2 + e % 2, i * D:(i + 1) * D],
                                gates[0:TILE, x, i, e:e + 1], h[0:TILE, x, i], ALU.mult, ALU.add)
                        last.then_inc(S["gated"], 1)
                    yield

            run_all(softmax_attention, linear_and_causal_attention, experts, n)

        @block.tensor
        def _(pe):
            n = Counter(pe, "wait_pe")
            def mm3(out, a, b, start=True, stop=True, skip=False):
                (ah, al), (bh, bl) = a, b
                nc.tensor.matmul(out, ah, bh, start=start, stop=False, skip_group_check=skip)
                nc.tensor.matmul(out, ah, bl, start=False, stop=False, skip_group_check=skip)
                return nc.tensor.matmul(out, al, bh, start=False, stop=stop, skip_group_check=skip)

            pe.wait_ge(started, 1)
            pe.wait_ge(consts_built, 1)
            pe.wait_ge(w_lo_done, 1)

            def turn_input(k, u):
                p = k * 2 + u
                pe.wait_ge(x_loaded[u], n.plain((k + 1) * 32))
                pe.wait_ge(x_lo_done, n(p - 1))
                for i in range(4):
                    last = nc.tensor.transpose(pf[0:CHANNELS, u, i * 128:(i + 1) * 128],
                                               fs[:, u, i * CHANNELS:(i + 1) * CHANNELS], ident[:])
                last.then_inc(x_turned, 1)

            def taps(k, u):
                p = k * 2 + u
                pe.wait_ge(x_lo_done, n(p + 1))
                pe.wait_ge(y_ready, n(p - 1))
                for c in range(TAPS):
                    xs = [v[0:CHANNELS, u, :].rearrange("p (b l) -> p b l", b=2)[:, :, c:c + SEQ]
                          for v in (xf_hi, xf_lo)]
                    last = mm3(pf[:, 2 + u, 0:TOK].rearrange("p (b l) -> p b l", b=2), W("tok", c * D, D, CHANNELS),
                               xs, c == 0, c == TAPS - 1)
                last.then_inc(y_pre, 1)

            turn_input(0, 0)
            with n.loop(PAIRS // 2 - 1) as k:
                turn_input(k, 1)
                taps(k, 0)
                turn_input(k + 1, 0)
                taps(k, 1)
            turn_input(PAIRS // 2 - 1, 1)
            taps(PAIRS // 2 - 1, 0)
            taps(PAIRS // 2 - 1, 1)
            pe.wait_ge(bn_step, 5)

            def turn(t, src, step=None):
                pe.wait_ge(S["hi_ready"], n(t))
                pe.wait_ge(S["lo_ready"], n(t))
                for i in range(TILES):
                    last = nc.tensor.transpose(pa[:, 1, tile_cols(i)], src[0:TILE, i], ident[0:TILE, 0:TILE])
                last.then_inc(S["turned"], 1)

            def halves_ready(t):
                pe.wait_ge(S["hi_ready"], n(t + 1))
                pe.wait_ge(S["lo_ready"], n(t + 1))

            def spread_queries(f):
                for g in range(GROUPS):
                    nc.tensor.matmul(pa[:, g, 0:TOK], pick_q_hi[:, g], qk_hi[:, 0], start=True, stop=False)
                    nc.tensor.matmul(pa[:, g, 0:TOK], pick_q_lo[:, g], qk_lo[:, 0], start=False,
                                     stop=True).then_inc(S["spread"], 1)

            def spread_keys(f):
                for g in range(GROUPS):
                    pe.wait_ge(S["q_spread"], n(f * 4 + g + 1))
                    nc.tensor.matmul(pa[:, g, 0:TOK], pick_k_hi[:, g], qk_hi[:, 1], start=True, stop=False)
                    nc.tensor.matmul(pa[:, g, 0:TOK], pick_k_lo[:, g], qk_lo[:, 1], start=False,
                                     stop=True).then_inc(S["spread"], 1)

            def gate(f, x, kind):
                for i in range(TILES):
                    xs = (xf_hi[:, x, tile_cols(i)], xf_lo[:, x, tile_cols(i)])
                    last = mm3(pa[0:TILE, 2, i * EXPERTS:(i + 1) * EXPERTS], xs,
                               W(("gate0", "gate1")[kind], 0, EXPERTS))
                last.then_inc(S["logit_ready"], 1)
                yield
                pe.wait_ge(S["gate_ready"], n(f + 1))
                for i in range(TILES):
                    last = nc.tensor.transpose(pa[0:EXPERTS, 3, tile_cols(i)], gates[0:TILE, x, i],
                                               ident[0:TILE, 0:TILE])
                last.then_inc(S["gate_turned"], 1)
                yield
                pe.wait_ge(S["gate_t_ready"], n(f + 1))
                for i in range(TILES):
                    last = nc.tensor.matmul(pa[0:TILE, 0, i * D:(i + 1) * D], gate_t[:, tile_cols(i)],
                                            b2[:, kind], start=True, stop=True)
                last.then_inc(S["bias2_ready"], 1)
                yield

            def softmax_attention(k, x):
                p, f, t = phase_of("A0", k, x)
                yield
                pe.wait_ge(S["z_ready"], n(p + 1))
                pe.wait_ge(S["h_biased"], n(f))
                for i in range(TILES):
                    last = nc.tensor.transpose(pa[0:TILE, 0, i * D:(i + 1) * D], fs[:, 0, tile_cols(i)], ident[:])
                last.then_inc(S["z_turned"], 1)
                yield
                pe.wait_ge(S["xn_ready"], n(f * 2 + 1))
                turn(t, xn)
                yield
                halves_ready(t)
                xt = (xt_hi[:], xt_lo[:])
                pe.wait_ge(S["h_ready"], n(p + 1))
                mm3(pa[:, 0, 0:TOK], W("wq0", 0, D), xt).then_inc(S["q_proj"], 1)
                mm3(pa[:, 2, 0:TOK], W("wk0", 0, D), xt).then_inc(S["k_proj"], 1)
                for i in range(TILES):
                    last = mm3(pa[0:TILE, 3, i * D:(i + 1) * D],
                               (xt_hi[:, tile_cols(i)], xt_lo[:, tile_cols(i)]), W("wv0", 0, D))
                last.then_inc(S["v_proj"], 1)
                yield
                pe.wait_ge(S["qk_lo_ready"], n(p * 2 + 2))
                pe.wait_ge(S["v_ready"], n(p + 1))
                spread_queries(f)
                yield
                spread_keys(f)
                yield
                pe.wait_ge(S["k_spread"], n(f * 4 + 4))
                for i in range(16):
                    if i and i % 4 == 0:
                        yield
                    b, hd = i // HEADS, i % HEADS
                    rows_ = slice(64 * (hd % 2), 64 * (hd % 2) + 64)
                    if i >= 2:
                        pe.wait_ge(S["s_max"], n(p * 16 + i - 1))
                    for j in range(2):
                        last = nc.tensor.matmul(pa[0:TILE, i % 2, j * SEQ:(j + 1) * SEQ],
                                                q16[rows_, hd // 2, tile_cols(2 * b + j)],
                                                k16[rows_, hd // 2, b * SEQ:(b + 1) * SEQ], start=True, stop=True)
                    last.then_inc(S["s_raw"], 1)
                yield
                pe.wait_ge(S["s_max"], n(p * 16 + 16))
                for g in range(GROUPS):
                    if g >= 2:
                        pe.wait_ge(S["q_shifted"], n(p * 4 + g - 1))
                    for i in range(TILES):
                        last = nc.tensor.matmul(pa[:, 2 + g % 2, tile_cols(i)], minus_max[0:TILE, i, g],
                                                ident16[0:TILE, 0:TILE], start=True, stop=True)
                    last.then_inc(S["max_turned"], 1)
                yield
                pe.wait_ge(S["q_shifted"], n(p * 4 + 4))
                for i in range(18):
                    if i and i % 4 == 0:
                        yield
                    if i < 16:
                        b, hd = i // HEADS, i % HEADS
                        rows_ = slice(64 * (hd % 2), 64 * (hd % 2) + 64)
                        if i >= 2:
                            pe.wait_ge(S["p_exp"], n(p * 16 + i - 1))
                        for j in range(2):
                            last = nc.tensor.matmul(pa[0:TILE, i % 2, j * SEQ:(j + 1) * SEQ],
                                                    k16[rows_, hd // 2, tile_cols(2 * b + j)],
                                                    q16[rows_, hd // 2, b * SEQ:(b + 1) * SEQ],
                                                    start=True, stop=True)
                        last.then_inc(S["st_ready"], 1)
                    if i >= 2:
                        b, hd = (i - 2) // HEADS, (i - 2) % HEADS
                        pe.wait_ge(S["p_band"], n(p * 16 + i - 1))
                        for j in range(2):
                            first = (j * HEADS + hd) * (HEAD + 1)
                            for kt in range(2):
                                c0 = kt * SEQ + j * TILE
                                last = nc.tensor.matmul(pa[0:TILE, 2 + b, first:first + HEAD + 1],
                                                        pt[0:TILE, (i - 2) % 3, c0:c0 + TILE],
                                                        v0[0:TILE, 2 * b + kt, hd], start=(kt == 0), stop=(kt == 1))
                        last.then_inc(S["pv_done"], 1)
                yield
                pe.wait_ge(S["o_ready"], n(p * 2 + 2))
                turn(t + 1, xn)
                yield
                halves_ready(t + 1)
                for i in range(TILES):
                    last = mm3(pa[0:TILE, 0, i * D:(i + 1) * D],
                               (ot_hi[0][:, tile_cols(i)], ot_lo[0][:, tile_cols(i)]), W("wo0", 0, D))
                last.then_inc(S["wo_ready"], 1)
                yield
                pe.wait_ge(S["xn_ready"], n(f * 2 + 2))
                turn(t + 2, xn)
                yield
                yield
                halves_ready(t + 2)
                yield from gate(f, x, 0)

            def linear_and_causal_attention(k, x):
                p, f, t = phase_of("A1", k, x)
                yield
                pe.wait_ge(S["xn_ready"], n(f * 2 + 1))
                pe.wait_ge(S["h_biased"], n(f))
                turn(t, xn)
                yield
                halves_ready(t)
                xt = (xt_hi[:], xt_lo[:])
                mm3(pa[:, 0, 0:TOK], W("wq1", 0, D), xt).then_inc(S["q_proj"], 1)
                mm3(pa[:, 2, 0:TOK], W("wk1", 0, D), xt).then_inc(S["k_proj"], 1)
                yield
                for i in range(TILES):
                    if i >= 2:
                        pe.wait_ge(S["v1_ready"], n(p * 4 + i - 1))
                    mm3(pa[0:TILE, (3, 1)[i % 2], 0:HEADS * LIN_VALUE],
                        (xt_hi[:, tile_cols(i)], xt_lo[:, tile_cols(i)]),
                        W("wv1", 0, HEADS * LIN_VALUE)).then_inc(S["v1_proj"], 1)
                yield
                pe.wait_ge(S["qk_lo1"], n(p * 2 + 2))
                pe.wait_ge(S["v1_ready"], n(p * 4 + 4))
                spread_queries(f)
                yield
                spread_keys(f)
                yield
                pe.wait_ge(S["k_spread"], n(f * 4 + 4))
                for i in range(18):
                    if i and i % 4 == 0:
                        yield
                    if i < 16:
                        b, hd = i // HEADS, i % HEADS
                        rows_ = slice(64 * (hd % 2), 64 * (hd % 2) + 64)
                        if i >= 2:
                            pe.wait_ge(S["at_ready"], n(p * 16 + i - 1))
                        nc.tensor.matmul(pa[0:TILE, i % 2, 0:SEQ], k16[rows_, hd // 2, tile_cols(2 * b)],
                                         q16[rows_, hd // 2, b * SEQ:(b + 1) * SEQ], start=True, stop=True)
                        nc.tensor.matmul(pa[0:TILE, i % 2, SEQ:SEQ + TILE],
                                         k16[rows_, hd // 2, tile_cols(2 * b + 1)],
                                         q16[rows_, hd // 2, tile_cols(2 * b + 1)],
                                         start=True, stop=True).then_inc(S["at_raw"], 1)
                    if i >= 2:
                        j = i - 2
                        b, hd, g8 = j // HEADS, j % HEADS, j // 2
                        pe.wait_ge(S["at_ready"], n(p * 16 + j + 1))
                        if j % 2 == 0 and g8 >= 2:
                            pe.wait_ge(S["o1_norm"], n(p * 8 + g8 - 1))
                        wide = LIN_VALUE + 1
                        for qt, blocks in ((0, ((0, 0),)), (1, ((0, 1), (1, 2)))):
                            first = (2 * (hd % 2) + qt) * wide
                            for m, (kt, block_) in enumerate(blocks):
                                last = nc.tensor.matmul(pa[0:TILE, 2 + g8 % 2, first:first + wide],
                                                        pt[0:TILE, j % 3, tile_cols(block_)],
                                                        v1[0:TILE, 2 * b + kt, hd], start=(m == 0),
                                                        stop=(m == len(blocks) - 1))
                        last.then_inc(S["av_done"], 1)
                yield
                for c in range(5):
                    if c < 4:
                        if c == 0:
                            pe.wait_ge(S["o1_norm"], n(p * 8 + 8))
                        turn(t + 1 + c, o1_rows[:, :, c * 128:(c + 1) * 128])
                    if c >= 1:
                        halves_ready(t + c)
                        for i in range(TILES):
                            last = mm3(pa[0:TILE, 0, i * D:(i + 1) * D],
                                       (ot_hi[(c - 1) % 2][:, tile_cols(i)], ot_lo[(c - 1) % 2][:, tile_cols(i)]),
                                       W("wo1", (c - 1) * D, D), c == 1 and i == 0, c == 4 and i == 3, True)
                    if c == 4:
                        last.then_inc(S["wo1_ready"], 1)
                    yield
                pe.wait_ge(S["xn_ready"], n(f * 2 + 2))
                turn(t + 5, xn)
                yield
                halves_ready(t + 5)
                for i in range(TILES):
                    mm3(pa[0:TILE, (0, 2, 3, 1)[i], 0:3 * D], (xt_hi[:, tile_cols(i)], xt_lo[:, tile_cols(i)]),
                        W("wqkv2", 0, 3 * D)).then_inc(S["qkv_proj"], 1)
                yield
                yield
                pe.wait_ge(S["qkn_ready"], n(p + 1))
                for j, bank in ((0, 0), (1, 2)):
                    for i in range(TILES):
                        last = nc.tensor.transpose(pa[:, bank, tile_cols(i)], qkv[0:TILE, i, j * D:(j + 1) * D],
                                                   ident[0:TILE, 0:TILE])
                    last.then_inc(S["qk2_turned"], 1)
                yield
                pe.wait_ge(S["q2_ready"], n(p + 1))
                pe.wait_ge(S["k2_ready"], n(p + 1))
                for i in range(6):
                    if i < 4:
                        b, hd = i // 2, i % 2
                        rows_ = slice(64 * hd, 64 * hd + 64)
                        pe.wait_ge(S["s2_masked"], n(p * 4 + i - 1))
                        bank = pa[0:TILE, 2 * (i % 2)]
                        nc.tensor.matmul(bank[:, 0:TILE], q2t[rows_, tile_cols(2 * b)],
                                         k2t[rows_, tile_cols(2 * b)], start=True, stop=True)
                        nc.tensor.matmul(bank[:, TILE:3 * TILE], q2t[rows_, tile_cols(2 * b + 1)],
                                         k2t[rows_, b * SEQ:(b + 1) * SEQ], start=True,
                                         stop=True).then_inc(S["s2_raw"], 1)
                    if 1 <= i <= 4:
                        j = i - 1
                        pe.wait_ge(S["p2_ready"], n(p * 4 + j + 1))
                        pe.wait_ge(S["p2t_ready"], n(p * 4 + j))
                        for blk in range(3):
                            last = nc.tensor.transpose(pa[0:TILE, 1, tile_cols(blk)], pt[0:TILE, j % 2, tile_cols(blk)],
                                                       ident[0:TILE, 0:TILE])
                        last.then_inc(S["p2_turned"], 1)
                    if i >= 2:
                        j = i - 2
                        b, hd = j // 2, j % 2
                        pe.wait_ge(S["p2t_ready"], n(p * 4 + j + 1))
                        for qt, blocks in ((0, ((0, 0),)), (1, ((0, 1), (1, 2)))):
                            first = ((2 * b + qt) * HEADS2 + hd) * HEAD2
                            for m, (kt, blk) in enumerate(blocks):
                                c0 = 2 * D + hd * HEAD2
                                last = nc.tensor.matmul(pa[0:TILE, 3, first:first + HEAD2],
                                                        fs[0:TILE, j % 2, tile_cols(blk)],
                                                        qkv[0:TILE, 2 * b + kt, c0:c0 + HEAD2], start=(m == 0),
                                                        stop=(m == len(blocks) - 1))
                        last.then_inc(S["pv2_done"], 1)
                    yield
                pe.wait_ge(S["o2_ready"], n(p + 1))
                turn(t + 6, xn)
                yield
                halves_ready(t + 6)
                mm3(pa[:, 0, 0:TOK], W("wo2", 0, D), (ot_hi[0], ot_lo[0])).then_inc(S["y_proj"], 1)
                yield
                pe.wait_ge(S["y_hi"], n(p + 1))
                pe.wait_ge(S["y_lo"], n(p + 1))
                yield from gate(f, x, 1)

            def experts(kind, k, x):
                experts_before, before = chunks_before(kind, k, x)
                half = half_of(kind, k, x)
                per = (CHUNKS0, CHUNKS1)[kind]
                up, down = (("up0", "down0"), ("up1", "down1"))[kind]
                total = EXPERTS * per
                for c in range(total + LAG):
                    if c < total:
                        pe.wait_ge(S["hid_ready"], n(before + c - 1))
                        mm3(pf[:, c % 2, 0:TOK], W(up, c * 128, 128),
                            (xf_hi[:, x, 0:TOK], xf_lo[:, x, 0:TOK])).then_inc(S["pre_ready"], 1)
                    if c >= LAG:
                        j = c - LAG
                        e, m = j // per, j % per
                        pe.wait_ge(S["hid_hi_done"], n(before + j + 1))
                        pe.wait_ge(hid_lo_done[j % 2], n(half + j // 2 + 1))
                        if m == 0:
                            pe.wait_ge(S["gated"], n(experts_before + e - 1))
                        for i in range(TILES):
                            last = mm3(pf[0:TILE, 2 + e % 2, i * D:(i + 1) * D],
                                       (hid_hi[:, j % 4, tile_cols(i)], hid_lo[:, j % 4, tile_cols(i)]),
                                       W(down, j * D, D), m == 0 and i == 0, m == per - 1 and i == 3, True)
                        last.then_inc(S["hid_used"], 1)
                    yield

            run_all(softmax_attention, linear_and_causal_attention, experts, n)


def kernel(**inputs):
    import numpy as _np
    import concourse.bacc as _bacc
    from concourse import mybir as _mybir
    from concourse.bass_utils import run_bass_kernel_spmd as _run

    a = {name: _np.asarray(value) for name, value in inputs.items()}

    def taps_first():
        w = a["L0_tok_W"].reshape(D, TAPS, CHANNELS).transpose(2, 1, 0).reshape(CHANNELS, TAPS * D)
        return _np.concatenate([w, _np.zeros((128 - CHANNELS, TAPS * D), w.dtype)], 0)

    def by_chunk(w):
        e, f, d = w.shape
        return w.reshape(e, f // 128, 128, d).transpose(2, 0, 1, 3).reshape(128, -1)

    def inputs_first(w):
        return w.transpose(1, 0, 2).reshape(D, -1)

    weights = {
        "tok": taps_first(),
        "wq0": a["L0_attn_Wq"].T, "wk0": a["L0_attn_Wk"].T, "wv0": a["L0_attn_Wv"].T, "wo0": a["L0_attn_Wo"].T,
        "wq1": a["L1_attn_W_q"].T, "wk1": a["L1_attn_W_k"].T, "wv1": a["L1_attn_W_v"].T,
        "wo1": a["L1_attn_W_out"].T.reshape(HEADS * LIN_VALUE // 128, 128, D).transpose(1, 0, 2).reshape(128, -1),
        "wqkv2": _np.concatenate([a["L1_ffn_Wq"], a["L1_ffn_Wk"], a["L1_ffn_Wv"]], 1), "wo2": a["L1_ffn_Wo"],
        "gate0": a["L0_ffn_Wr"].T, "gate1": a["L1_ffn_gate_W"],
        "up0": inputs_first(a["L0_ffn_W1"]), "down0": by_chunk(a["L0_ffn_W2"]),
        "up1": inputs_first(a["L1_ffn_W1"]), "down1": by_chunk(a["L1_ffn_W2"]),
    }
    columns = [a["L0_tok_b"], a["L0_tok_gamma"], a["L0_tok_beta"], a["L0_attn_bq"], a["L0_attn_ocr_bias"],
               a["L0_attn_bk"], a["L1_ffn_ln_g"], a["L1_ffn_ln_b"], _np.tile(a["L1_ffn_qn_g"], HEADS2),
               _np.tile(a["L1_ffn_kn_g"], HEADS2), *a["L0_ffn_b1"].reshape(-1, 128), *a["L1_ffn_b1"].reshape(-1, 128)]
    arrays = {
        "x": a["x"],
        "weights": _np.concatenate([weights[name] for name, _ in WIDTHS], 1),
        "vectors": _np.stack(columns, 1),
        "rows": _np.concatenate([a["L0_attn_bv"], a["L0_attn_bo"], a["L0_ffn_br"], a["L1_ffn_gate_b"]]),
        "b2": _np.stack([a["L0_ffn_b2"], a["L1_ffn_b2"]], 1),
    }
    nc = _bacc.Bacc("TRN2", target_bir_lowering=False, num_devices=1)
    arrays = {f"in_{name}": _np.ascontiguousarray(v) for name, v in arrays.items()}
    args = [nc.dram_tensor(name, v.shape, _mybir.dt.from_np(v.dtype), kind="ExternalInput").ap()
            for name, v in arrays.items()]
    args.append(nc.dram_tensor("out", (BATCH, SEQ, D), F32, kind="ExternalOutput").ap())
    program(nc, *args)
    return _run(nc, [arrays], core_ids=[0]).results[0]["out"]
```

```python
from contextlib import ExitStack, contextmanager

import numpy as np

import concourse.bass as bass
from concourse import mybir

ALU = mybir.AluOpType
ACT = mybir.ActivationFunctionType
AX = mybir.AxisListType
F32 = mybir.dt.float32
F16 = mybir.dt.float16

BATCH, LENGTH, CHANNELS = 64, 256, 80
TAPS = 5
SEQ = LENGTH - TAPS + 1
D = 128
TILE = SEQ // 2
TILES = 4
TOK = TILES * TILE
PAIRS = BATCH // 2
HEADS, HEAD = 8, 16
GROUPS = HEADS // 2
LIN_VALUE = 64
HEADS2, HEAD2 = 2, 64
EXPERTS = 8
CHUNKS0, CHUNKS1 = 2, 4
EPS = 1e-5
BAND, BAND_WIDTH = 5, 131
POOL_EVEN = True
HIDS = 2
LAG = 4

WIDTHS = [("tok", TAPS * D), ("wq0", D), ("wk0", D), ("wv0", D), ("wo0", D),
          ("wq1", D), ("wk1", D), ("wv1", HEADS * LIN_VALUE), ("wo1", HEADS * LIN_VALUE),
          ("wqkv2", 3 * D), ("wo2", D), ("gate0", EXPERTS), ("gate1", EXPERTS),
          ("up0", EXPERTS * CHUNKS0 * 128), ("down0", EXPERTS * CHUNKS0 * D),
          ("up1", EXPERTS * CHUNKS1 * 128), ("down1", EXPERTS * CHUNKS1 * D)]
COL, NCOL = {}, 0
for _name, _width in WIDTHS:
    COL[_name] = NCOL
    NCOL += _width
PIECES = 8
PIECE = NCOL // PIECES
assert PIECE * PIECES == NCOL and PIECE <= TILES * HEADS * LIN_VALUE
V_TOKB, V_GAMMA, V_BETA, V_BQ, V_OCR, V_BK, V_LNG, V_LNB, V_QN, V_KN = range(10)
V_B0 = 10
V_B1 = V_B0 + EXPERTS * CHUNKS0
NVEC = V_B1 + EXPERTS * CHUNKS1
R_BV, R_BO, R_G0, R_G1 = 0, D, 2 * D, 2 * D + EXPERTS
NROW = 2 * D + 2 * EXPERTS

START = 8


class Count:

    def __init__(self, per_round, offset):
        self.per_round, self.offset = per_round, offset

    def __add__(self, other):
        if isinstance(other, Count):
            return Count(self.per_round + other.per_round, self.offset + other.offset)
        return Count(self.per_round, self.offset + other)

    __radd__ = __add__

    def __sub__(self, other):
        return self + -1 * other

    def __mul__(self, factor):
        return Count(self.per_round * factor, self.offset * factor)

    __rmul__ = __mul__


class Counter:

    def __init__(self, engine, name):
        self.engine, self.round, self.multiples = engine, None, {}
        self.value = engine.alloc_register(name)

    @contextmanager
    def loop(self, rounds):
        with self.engine.Fori(0, rounds) as k:
            self.round, self.multiples = k, {}
            yield Count(1, 0)
            self.round = None

    def plain(self, count):
        if not isinstance(count, Count):
            return count
        if count.per_round == 0:
            return count.offset
        if count.per_round not in self.multiples:
            self.multiples[count.per_round] = self.engine.snap(self.round * count.per_round)
        self.engine.reg_add(self.value, self.multiples[count.per_round], count.offset)
        return self.value

    def __call__(self, count):
        return self.plain(count + START)

    def index(self, count):
        if not isinstance(count, Count) or count.per_round == 0:
            return count.offset if isinstance(count, Count) else count
        return self.round * count.per_round + count.offset



def before_first(p):
    if not isinstance(p, Count):
        return p, max(p - 1, 0)
    return p, p - 1


def before_second(p):
    if not isinstance(p, Count):
        return min(p + 2, PAIRS), p
    return p + 2, p


def chunks_before(kind, p):
    first, second = (before_first, before_second)[kind](p)
    return (first + second) * EXPERTS, first * (EXPERTS * CHUNKS0) + second * (EXPERTS * CHUNKS1)


def halves_before(kind, p):
    first, second = (before_first, before_second)[kind](p)
    return first * (EXPERTS * CHUNKS0 // 2) + second * (EXPERTS * CHUNKS1 // 2)


SLOTS = 2 * EXPERTS * (CHUNKS0 + CHUNKS1)
QK_STEPS, A0_STEPS, A1_STEPS = 9, 32, 49


def spread(begin, over, *paces):
    weights = [weight for steps, weight in paces for _ in range(steps)]
    return [begin + sum(weights[:i]) * over // sum(weights) for i in range(len(weights))]


QK_AT = spread(66, 30, (9, 4))
A0_AT = spread(0, 66, (9, 4), (11, 4), (12, 4))
A1_AT = spread(0, 94, (9, 4), (13, 4), (7, 4), (7, 4), (6, 4), (7, 4))
assert (len(QK_AT), len(A0_AT), len(A1_AT)) == (QK_STEPS, A0_STEPS, A1_STEPS)


def weave(slots, *parts):
    done = [0] * len(parts)
    for i in range(slots):
        for j, (at, part) in enumerate(parts):
            while done[j] < len(at) and at[done[j]] <= i:
                next(part)
                done[j] += 1


def chunks_of(kind, p):
    return [(kind, p, c) for c in range(EXPERTS * (CHUNKS0, CHUNKS1)[kind])]


def mixture(hidden, output, first, second):
    for a, b in zip(first, second, strict=True):
        if a:
            hidden(*a)
        yield
        if b:
            output(*b)
        yield


def run_rounds(queries_and_keys, first_attention, second_attention, hidden, output, n):
    later = [None] * LAG

    def body(r, start_next):
        mixtures = mixture(hidden, output, chunks_of(1, r - 1)[LAG:] + chunks_of(0, r + 1) + chunks_of(1, r)[:LAG],
                           chunks_of(1, r - 1) + chunks_of(0, r + 1))
        parts = [(range(SLOTS), mixtures), (A0_AT, first_attention(r + 1)), (A1_AT, second_attention(r))]
        if start_next:
            parts.append((QK_AT, queries_and_keys(r + 2)))
        weave(SLOTS, *parts)

    def first_body():
        linear = second_attention(0)
        share = A0_STEPS // 2
        weave(A0_STEPS, (range(share, A0_STEPS), linear), (range(A0_STEPS), first_attention(1)))
        slots = 2 * (EXPERTS * CHUNKS0 + LAG)
        mixtures = mixture(hidden, output, chunks_of(0, 1) + chunks_of(1, 0)[:LAG], later + chunks_of(0, 1))
        weave(slots, (range(slots), mixtures), (spread(0, slots - 6, (A1_STEPS - share, 1)), linear),
              (spread(0, slots, (QK_STEPS, 1)), queries_and_keys(2)))

    def last_body():
        r = PAIRS - 1
        linear = second_attention(r)
        slots = 2 * EXPERTS * CHUNKS1
        mixtures = mixture(hidden, output, chunks_of(1, r - 1)[LAG:] + later, chunks_of(1, r - 1))
        weave(slots, (range(slots), mixtures), (spread(0, slots, (A1_STEPS - 3, 1)), linear))
        for _ in linear:
            pass

    def alone(kind, p):
        chunks = chunks_of(kind, p)
        slots = 2 * (len(chunks) + LAG)
        parts = [(range(slots), mixture(hidden, output, chunks + later, later + chunks))]
        if kind == 0:
            parts.append((spread(0, slots, (QK_STEPS, 1)), queries_and_keys(p + 1)))
        weave(slots, *parts)

    for part in (queries_and_keys(0), first_attention(0)):
        for _ in part:
            pass
    alone(0, 0)
    first_body()
    with n.loop(PAIRS - 3) as k:
        body(k + 1, True)
    body(PAIRS - 2, False)
    last_body()
    alone(1, PAIRS - 1)


def program(nc, x_dram, w_dram, vec_dram, row_dram, b2_dram, out_dram):
    y_dram = nc.dram_tensor("y_scratch", (PAIRS, 128, TOK), F32, kind="Internal").ap()
    with ExitStack() as ctx:
        def sb(name, shape, dt=F32):
            return ctx.enter_context(nc.sbuf_tensor(name, shape, dt))

        def sem(name):
            return ctx.enter_context(nc.semaphore(name))

        w_hi = sb("w_hi", [128, NCOL], F16)
        w_lo = sb("w_lo", [128, NCOL], F16)
        vec = sb("vec", [128, NVEC])
        rows = sb("rows", [128, NROW])
        b2 = sb("b2", [EXPERTS, 2, D])
        ident = sb("ident", [128, 128])
        ident16 = sb("ident16", [128, 128], F16)
        pick_q_hi = sb("pick_q_hi", [128, GROUPS, 128], F16)
        pick_q_lo = sb("pick_q_lo", [128, GROUPS, 128], F16)
        pick_k_hi = sb("pick_k_hi", [128, GROUPS, 128], F16)
        pick_k_lo = sb("pick_k_lo", [128, GROUPS, 128], F16)
        one_row = sb("one_row", [128, 1])
        band = sb("band", [128, 2, BAND_WIDTH])
        causal = sb("causal", [128, 3, TILE])
        causal_add = sb("causal_add", [128, 3, TILE])
        earlier = sb("earlier", [128, EXPERTS, EXPERTS])
        minus_half = sb("minus_half", [128, 16])
        q_bias = sb("q_bias", [128, 1])
        qk_gain = sb("qk_gain", [128, 1])
        bn_part = sb("bn_part", [128, PAIRS * 6])
        bn = sb("bn", [128, 2])
        bn_var = sb("bn_var", [128, 1])
        bn_rstd = sb("bn_rstd", [128, 1])
        bn_scale = sb("bn_scale", [128, 1])
        bn_shift = sb("bn_shift", [128, 1])
        ha = sb("ha", [128, TILES, D])
        h0 = sb("h0", [128, TILES, D])
        h1 = sb("h1", [128, TILES, D])
        h2 = sb("h2", [128, TILES, D])
        h_of = (h0, h2)
        xf_hi = sb("xf_hi", [128, 2, 512], F16)
        xf_lo = sb("xf_lo", [128, 2, 512], F16)
        gates = sb("gates", [128, 2, TILES, EXPERTS])
        hid = sb("hid", [128, HIDS, TOK])
        hid_hi = sb("hid_hi", [128, 8, TOK], F16)
        hid_lo = sb("hid_lo", [128, 8, TOK], F16)
        fs1 = sb("fs1", [128, 2, 512])
        ts = [sb(f"ts{i}", [128, 512]) for i in range(2)]
        xn = [sb(f"xn{i}", [128, TILES, D]) for i in range(2)]
        xt_hi = [sb(f"xt_hi{i}", [128, TOK], F16) for i in range(2)]
        xt_lo = [sb(f"xt_lo{i}", [128, TOK], F16) for i in range(2)]
        ot_hi = [sb(f"ot_hi{i}", [128, 1 + i, TOK], F16) for i in range(2)]
        ot_lo = [sb(f"ot_lo{i}", [128, 1 + i, TOK], F16) for i in range(2)]
        qk_hi = [sb(f"qk_hi{i}", [128, 2, TOK], F16) for i in range(2)]
        qk_lo = [sb(f"qk_lo{i}", [128, 2, TOK], F16) for i in range(2)]
        q16 = [sb(f"q_spread{i}", [128, GROUPS, TOK], F16) for i in range(2)]
        k16 = [sb(f"k_spread{i}", [128, GROUPS, TOK], F16) for i in range(2)]
        pt = [sb("pt0", [128, 8, TOK]), sb("pt1", [128, 4, TOK])]
        st = [sb(f"st{i}", [128, TILES, 6]) for i in range(2)]
        mv = [sb(f"mv{i}", [128, TILES, 2]) for i in range(2)]
        ve = [sb(f"ve{i}", [128, TILES]) for i in range(2)]
        rstd = [sb(f"rstd{i}", [128, TILES]) for i in range(2)]
        lg = [sb(f"lg{i}", [128, TILES, EXPERTS]) for i in range(2)]
        lge = [sb(f"lge{i}", [128, TILES, EXPERTS]) for i in range(2)]
        lmax = [sb(f"lmax{i}", [128, TILES]) for i in range(2)]
        lsum = [sb(f"lsum{i}", [128, TILES]) for i in range(2)]
        gate_t = [sb(f"gate_t{i}", [EXPERTS, TOK]) for i in range(2)]
        y_in = sb("y_in", [128, TOK])
        v0 = sb("v0", [128, TILES, HEADS, HEAD + 1])
        minus_max = sb("minus_max", [128, TILES, GROUPS, 128], F16)
        rec = sb("rec", [128, 2, 16])
        v1 = sb("v1", [128, TILES, HEADS, LIN_VALUE + 1])
        o1 = sb("o1", [128, TILES, HEADS, LIN_VALUE])
        den = sb("den", [128, 2, 4])
        inv_den = sb("inv_den", [128, 2, 4])
        ss = sb("ss", [128, 16])
        ss_eps = sb("ss_eps", [128, 16])
        inv_norm = sb("inv_norm", [128, 16])
        row_max = sb("row_max", [128, 8])
        row_sum = sb("row_sum", [128, TILES, HEADS2])
        inv_sum = sb("inv_sum", [128, 8])

        pa0 = ctx.enter_context(nc.psum_tensor("pa0", [128, 3, 512], F32))
        pa1 = ctx.enter_context(nc.psum_tensor("pa1", [128, 2, 512], F32))
        pf = ctx.enter_context(nc.psum_tensor("pf", [128, 3, 512], F32))
        pa = (pa0, pa1)
        TURN = 1
        LOGITS, GATES_T, BIAS2 = (2, 1), (1, 0), (0, 1)

        q2t, k2t = pt[1][:, 0], pt[1][:, 1]
        p2 = (pt[1][:, 2], pt[1][:, 3], ts[1][:, 0:TOK], ts[0][:, 0:TOK])
        over = ts[0][:, 0:256].rearrange("p (t a b) -> p t a b", t=TILES, a=EXPERTS)
        same = ts[0][:, 256:512].rearrange("p (t a b) -> p t a b", t=TILES, a=EXPERTS)
        v1_flat, o1_flat = v1[:].rearrange("p t h d -> p (t h d)"), o1[:].rearrange("p t h d -> p (t h d)")
        qkv = v1_flat[:, 0:TILES * 3 * D].rearrange("p (t c) -> p t c", t=TILES)
        squares = o1_flat[:, 0:TILES * 2 * D].rearrange("p (t c) -> p t c", t=TILES)
        o1_rows = o1[:].rearrange("p t h d -> p t (h d)")
        staging = (v1_flat[:, 0:PIECE], o1_flat[:, 0:PIECE])
        y_tile = (hid[:, 0], hid[:, 1])
        x_in = (pt[0][:, 0], pt[0][:, 1])
        z = pt[0][:, 0]

        def W(name, first, width, rows_=128):
            c = COL[name] + first
            return w_hi[0:rows_, c:c + width], w_lo[0:rows_, c:c + width]

        def cols(t):
            return slice(t * TILE, (t + 1) * TILE)

        def by_tile(bank):
            return bank[0:TILE].rearrange("p (t d) -> p t d", t=TILES)

        def head_rows(hd):
            return slice(64 * (hd % 2), 64 * (hd % 2) + 64)

        started = sem("started")
        w_loaded = [sem(f"w_loaded{i}") for i in range(PIECES)]
        small_loaded = sem("small_loaded")
        const_done, consts_built = sem("const_done"), sem("consts_built")
        w_hi_done, w_lo_done, derived, bn_step = (sem(x) for x in ("w_hi_done", "w_lo_done", "derived", "bn_step"))
        x_loaded = [sem("x_loaded0"), sem("x_loaded1")]
        y_stored = [sem("y_stored0"), sem("y_stored1")]
        y_loaded = sem("y_loaded")
        out_sent = sem("out_sent")
        T = {name: sem(name) for name in "x_turned x_hi_done x_lo_done y_pre y_ready y_stats".split()}
        both = ("ln_stats ln_aggr var_ready rstd_ready xn_ready turned hi_ready lo_ready q_proj k_proj spread "
                "q_spread k_spread logit_ready l_biased l_max l_shifted l_exp l_sum l_rec gate_ready "
                "gate_turned gate_t_ready bias2_ready h_biased")
        S0 = {name: sem(name + "_0") for name in both.split()}
        S1 = {name: sem(name + "_1") for name in both.split()}
        SS = (S0, S1)
        for name in ("z_ready z_turned h_ready v_proj qk_hi_ready qk_lo_ready v_ready s_raw s_max max_turned "
                     "q_shifted st_ready p_exp p_band pv_done o_rec o_ready wo_ready h_bo h_attn probs "
                     "ranks1 ranks2 ranks3 ranks4 ranks5").split():
            S0[name] = sem(name)
        for name in ("carried el_exp el_min el_map el_hi el_lo v1_ones v1_proj v1_ready at_raw at_ready off_ready av_done "
                     "den_done den_rec o1_norm wo1_ready h_lin aff_ready qkv_proj qkv_ready sq_ready ss_sum "
                     "ss_ready rn_ready qkn_ready qk2_turned q2_ready k2_ready s2_raw s2_masked s2_max p2_ready "
                     "p2_turned p2t_ready pv2_done rs_rec o2_ready y_proj y_hi y_lo").split():
            S1[name] = sem(name)
        F = {name: sem(name) for name in "pre_ready hid_ready hid_hi_done hid_used gated".split()}
        hid_lo_done = [sem("hid_lo_even"), sem("hid_lo_odd")]
        from_start = [*T.values(), *S0.values(), *S1.values(), *F.values(), *hid_lo_done]

        block = ctx.enter_context(nc.Block())

        @block.sync
        def _(sp):
            n = Counter(sp, "wait_sp")
            for i in range(PIECES):
                if i >= 2:
                    sp.wait_ge(w_lo_done, i - 1)
                sp.dma_start(staging[i % 2], w_dram[:, i * PIECE:(i + 1) * PIECE]).then_inc(w_loaded[i], 16)
                if i == 0:
                    sp.dma_start(vec[:], vec_dram).then_inc(small_loaded, 16)
                    sp.dma_start(rows[:], row_dram.partition_broadcast(128)).then_inc(small_loaded, 16)
                    sp.dma_start(b2[:], b2_dram).then_inc(small_loaded, 16)
            sp.wait_ge(started, 1)

            def load_x(k, u):
                sp.wait_ge(T["x_turned"], n(k * 2 + u - 1))
                src = x_dram[bass.ds(n.index(k * 4 + 2 * u), 2)].rearrange("b (w l) c -> l b w c", w=2)
                dst = x_in[u][:, 0:TILES * CHANNELS].rearrange("p (b w c) -> p b w c", b=2, w=2)
                for b in range(2):
                    sp.dma_start(dst[:, b], src[:, b]).then_inc(x_loaded[u], 16)

            def store_y(k, u):
                sp.wait_ge(T["y_ready"], n(k * 2 + u + 1))
                sp.dma_start(y_dram[n.index(k * 2 + u)], y_tile[u]).then_inc(y_stored[u], 16)

            load_x(0, 0)
            load_x(0, 1)
            with n.loop(PAIRS // 2 - 1) as k:
                load_x(k + 1, 0)
                store_y(k, 0)
                load_x(k + 1, 1)
                store_y(k, 1)
            store_y(PAIRS // 2 - 1, 0)
            store_y(PAIRS // 2 - 1, 1)
            for u in range(2):
                sp.wait_ge(y_stored[u], 16 * (PAIRS // 2))

            def load_y(p):
                sp.wait_ge(S0["z_ready"], n(p))
                sp.dma_start(y_in[:], y_dram[n.index(p)]).then_inc(y_loaded, 16)

            def store_out(p):
                experts_before, _ = chunks_before(1, p)
                sp.wait_ge(F["gated"], n(experts_before + EXPERTS))
                dst = out_dram[bass.ds(n.index(p * 2), 2)].rearrange("b (t q) d -> q b t d", t=2)
                src = h2[0:TILE].rearrange("p (b t) d -> p b t d", b=2)
                for b in range(2):
                    sp.dma_start(dst[:, b], src[:, b]).then_inc(out_sent, 16)

            load_y(0)
            load_y(1)
            load_y(2)
            load_y(3)
            with n.loop(PAIRS - 4) as k:
                store_out(k)
                load_y(k + 4)
            for p in range(PAIRS - 4, PAIRS):
                store_out(p)
            sp.wait_ge(out_sent, 32 * PAIRS)

        @block.gpsimd
        def _(pool):
            n = Counter(pool, "wait_pool")
            for s in from_start:
                pool.sem_inc(s, START)
            pool.sem_inc(started, 1)
            steps = [0]

            def const(instruction):
                instruction.then_inc(const_done, 1)
                steps[0] += 1
                pool.wait_ge(const_done, steps[0])

            def keep(view, base, pattern, channel, fill, compare=ALU.is_ge):
                const(nc.gpsimd.affine_select(out=view, in_=view, compare_op=compare, fill=fill, base=base,
                                              pattern=pattern, channel_multiplier=channel))

            for view, value in ((ident[:], 0.0), (ident16[:], 0.0), (pick_q_hi[:], 0.0), (pick_q_lo[:], 0.0),
                                (pick_k_hi[:], 0.0), (pick_k_lo[:], 0.0), (one_row[:], 0.0),
                                (band[:], float(np.exp(np.float32(0.1)))), (causal[:], 1.0), (causal_add[:], 0.0),
                                (earlier[:], 1.0), (minus_half[:], -0.5), (v0[:], 1.0),
                                (minus_max[:], 0.0)):
                const(nc.gpsimd.memset(view, value))
            keep(ident[:], 0, [[-1, 128]], 1, 1.0, ALU.not_equal)
            keep(ident16[:], 0, [[-1, 128]], 1, 1.0, ALU.not_equal)
            for matrix, copies in ((pick_q_hi, (0, 1)), (pick_q_lo, (2,)), (pick_k_hi, (0, 2)), (pick_k_lo, (1,))):
                for g in range(GROUPS):
                    for r in copies:
                        view = matrix[:, g, :].rearrange("p (j r d) -> p j r d", j=2, d=HEAD)[:, :, r, :]
                        keep(view, -32 * g, [[-HEAD, 2], [-1, HEAD]], 1, 1.0, ALU.not_equal)
            keep(one_row[:], -48, [[0, 1]], 1, 1.0, ALU.not_equal)
            keep(one_row[:], -112, [[0, 1]], 1, 1.0, ALU.not_equal)
            keep(band[:], BAND, [[-5, 2], [1, BAND_WIDTH]], -1, 1.0)
            keep(band[:], BAND, [[5, 2], [-1, BAND_WIDTH]], 1, 1.0)
            for t in (0, 2):
                keep(causal[:, t, :], 0, [[1, TILE]], -1, 0.0)
                keep(causal_add[:, t, :], 0, [[-1, TILE]], 1, -1e30)
            keep(earlier[:], -1, [[1, EXPERTS], [-1, EXPERTS]], 0, 0.0)
            pool.sem_inc(consts_built, 1)
            pool.wait_ge(bn_step, 2)
            nc.gpsimd.tensor_tensor(bn_rstd[:], bn_var[:], minus_half[:, 0:1], ALU.pow).then_inc(bn_step, 1)

            def norm(a, count):
                pool.wait_ge(SS[a]["var_ready"], n(count + 1))
                nc.gpsimd.tensor_tensor(rstd[a][0:TILE], ve[a][0:TILE], minus_half[0:TILE, 0:TILES],
                                        ALU.pow).then_inc(SS[a]["rstd_ready"], 1)

            def softmax_queries_and_keys(p):
                yield
                yield
                yield
                norm(0, p * 2)
                for _ in range(6):
                    yield

            def softmax_attention(p):
                pool.wait_ge(S0["xn_ready"], n(p * 2 + 1))
                bo = rows[0:TILE, R_BO:R_BO + D].unsqueeze(1).to_broadcast([TILE, TILES, D])
                nc.gpsimd.tensor_tensor(ha[0:TILE], ha[0:TILE], bo, ALU.add).then_inc(S0["h_bo"], 1)
                for _ in range(9):
                    yield
                for g in range(8):
                    for i in (2 * g, 2 * g + 1):
                        pool.wait_ge(S0["p_exp"], n(p * 16 + i + 1))
                        strip = pt[0][0:TILE, i % 8, :]
                        strip = bass.AP(strip.tensor, strip.offset, [list(strip.ap[0]), [SEQ + TILE - BAND, 2],
                                                                     [1, BAND_WIDTH]])
                        nc.gpsimd.tensor_tensor(strip, strip, band[0:TILE], ALU.mult).then_inc(S0["p_band"], 1)
                    yield
                for _ in range(5):
                    yield
                norm(0, p * 2 + 1)
                for _ in range(10):
                    yield

            def linear_and_causal_attention(p):
                pool.wait_ge(S1["h_biased"], n(p))
                first, _ = chunks_before(0, p)
                counted = n(first + EXPERTS)
                pool.wait_ge(started, 1)
                pool.wait_ge(F["gated"], counted)
                nc.gpsimd.tensor_copy(h1[0:TILE], h0[0:TILE]).then_inc(S1["carried"], 1)
                norm(1, p * 2)
                yield
                yield
                counted = n(p)
                pool.wait_ge(started, 1)
                pool.wait_ge(S1["h_biased"], counted)
                nc.gpsimd.memset(v1[0:TILE, :, :, LIN_VALUE:LIN_VALUE + 1], 1.0).then_inc(S1["v1_ones"], 1)
                for _ in range(25):
                    yield
                norm(1, p * 2 + 1)
                for _ in range(4):
                    yield
                pool.wait_ge(S1["qkv_ready"], n(p * 4 + 4))
                nc.gpsimd.tensor_tensor(squares[0:TILE], qkv[0:TILE, :, 0:2 * D], qkv[0:TILE, :, 0:2 * D],
                                        ALU.mult).then_inc(S1["sq_ready"], 1)
                yield
                pool.wait_ge(S1["ss_ready"], n(p + 1))
                nc.gpsimd.tensor_tensor(inv_norm[0:TILE], ss_eps[0:TILE], minus_half[0:TILE, 0:16],
                                        ALU.pow).then_inc(S1["rn_ready"], 1)
                for _ in range(17):
                    yield

            def hidden(kind, p, c):
                _, before = chunks_before(kind, p)
                if c % 2 == 1 or POOL_EVEN:
                    pool.wait_ge(F["hid_hi_done"], n(before + c + 1))
                    nc.gpsimd.tensor_tensor(hid_lo[:, c % 8], hid[:, c % HIDS], hid_hi[:, c % 8],
                                            ALU.subtract).then_inc(hid_lo_done[c % 2], 1)

            def output(kind, p, j):
                pass

            run_rounds(softmax_queries_and_keys, softmax_attention, linear_and_causal_attention, hidden, output, n)

        @block.scalar
        def _(act):
            n = Counter(act, "wait_act")
            act.wait_ge(started, 1)
            for i in range(PIECES):
                act.wait_ge(w_loaded[i], 16)
                nc.scalar.copy(w_hi[:, i * PIECE:(i + 1) * PIECE], staging[i % 2]).then_inc(w_hi_done, 1)

            def high_of_input(k, u):
                p = k * 2 + u
                act.wait_ge(T["x_turned"], n(p + 1))
                act.wait_ge(T["y_pre"], n(p - 1))
                nc.scalar.copy(xf_hi[0:CHANNELS, u], pf[0:CHANNELS, u]).then_inc(T["x_hi_done"], 1)

            def relu(k, u):
                p = k * 2 + u
                act.wait_ge(T["y_pre"], n(p + 1))
                act.wait_ge(T["y_stats"], n(p - 1))
                act.wait_ge(y_stored[u], n.plain(k * 16))
                nc.scalar.activation(y_tile[u], pa0[:, u, 0:TOK], ACT.Relu,
                                     bias=vec[:, V_TOKB:V_TOKB + 1]).then_inc(T["y_ready"], 1)

            act.wait_ge(small_loaded, 48)
            high_of_input(0, 0)
            with n.loop(PAIRS // 2 - 1) as k:
                high_of_input(k, 1)
                relu(k, 0)
                high_of_input(k + 1, 0)
                relu(k, 1)
            high_of_input(PAIRS // 2 - 1, 1)
            relu(PAIRS // 2 - 1, 0)
            relu(PAIRS // 2 - 1, 1)

            def high(a, t, dst, scale=1.0, bias=0.0):
                act.wait_ge(SS[a]["turned"], n(t + 1))
                nc.scalar.activation(dst, pa[a][:, TURN, 0:TOK], ACT.Identity, scale=scale,
                                     bias=bias).then_inc(SS[a]["hi_ready"], 1)

            def spread_keys(a, p):
                for g in range(GROUPS):
                    bank = (GROUPS + g) % (3, 2)[a]
                    act.wait_ge(SS[a]["spread"], n(p * 8 + GROUPS + g + 1))
                    nc.scalar.activation(k16[a][:, g], pa[a][:, bank, 0:TOK], ACT.Identity,
                                         bias=one_row[:, 0:1]).then_inc(SS[a]["k_spread"], 1)

            def gate_exp(a, p):
                act.wait_ge(SS[a]["l_shifted"], n(p + 1))
                nc.scalar.activation(lge[a][0:TILE], lg[a][0:TILE], ACT.Exp).then_inc(SS[a]["l_exp"], 1)

            def gate(a, p):
                act.wait_ge(SS[a]["gate_turned"], n(p + 1))
                nc.scalar.copy(gate_t[a][:], pa[a][0:EXPERTS, GATES_T[a], 0:TOK]).then_inc(SS[a]["gate_t_ready"], 1)

            def softmax_queries_and_keys(p):
                yield
                yield
                yield
                act.wait_ge(S0["z_turned"], n(p + 1))
                act.wait_ge(S0["h_biased"], n(p))
                nc.scalar.copy(ha[0:TILE], by_tile(pa0[:, 0])).then_inc(S0["h_ready"], 1)
                yield
                yield
                high(0, p * 3, xt_hi[0][:])
                yield
                act.wait_ge(S0["q_proj"], n(p + 1))
                nc.scalar.activation(qk_hi[0][:, 0], pa0[:, 0, 0:TOK], ACT.Identity,
                                     bias=q_bias[:, 0:1]).then_inc(S0["qk_hi_ready"], 1)
                act.wait_ge(S0["k_proj"], n(p + 1))
                nc.scalar.activation(qk_hi[0][:, 1], pa0[:, 2, 0:TOK], ACT.Identity,
                                     bias=vec[:, V_BK:V_BK + 1]).then_inc(S0["qk_hi_ready"], 1)
                yield
                yield
                spread_keys(0, p)
                yield

            def softmax_attention(p):
                for _ in range(9):
                    yield
                for g in range(8):
                    for i in (2 * g, 2 * g + 1):
                        act.wait_ge(S0["st_ready"], n(p * 16 + i + 1))
                        act.wait_ge(S0["pv_done"], n(p * 16 + i - 7))
                        nc.scalar.activation(pt[0][0:TILE, i % 8], pa0[0:TILE, i % 2, 0:TOK], ACT.Exp,
                                             scale=HEAD ** -0.5).then_inc(S0["p_exp"], 1)
                    yield
                for _ in range(3):
                    yield
                high(0, p * 3 + 1, ot_hi[0][:, 0])
                yield
                for _ in range(3):
                    yield
                high(0, p * 3 + 2, xf_hi[:, 0, 0:TOK])
                yield
                yield
                gate_exp(0, p)
                for _ in range(3):
                    yield
                gate(0, p)
                yield
                yield
                yield

            def linear_and_causal_attention(p):
                yield
                yield
                high(1, p * 7, xt_hi[1][:])
                yield
                yield
                act.wait_ge(S1["q_proj"], n(p + 1))
                nc.scalar.activation(fs1[:, 0, 0:TOK], pa1[:, 0, 0:TOK], ACT.Exp).then_inc(S1["el_exp"], 1)
                act.wait_ge(S1["k_proj"], n(p + 1))
                nc.scalar.activation(fs1[:, 1, 0:TOK], pa1[:, 1, 0:TOK], ACT.Exp).then_inc(S1["el_exp"], 1)
                yield
                for tiles in ((0,), (1, 2), (3,)):
                    act.wait_ge(S1["v1_ones"], n(p + 1))
                    for i in tiles:
                        act.wait_ge(S1["v1_proj"], n(p * 4 + i + 1))
                        nc.scalar.copy(v1[0:TILE, i, :, 0:LIN_VALUE],
                                       pa1[0:TILE, i % 2].rearrange("p (h d) -> p h d", h=HEADS)
                                       ).then_inc(S1["v1_ready"], 1)
                    yield
                spread_keys(1, p)
                yield
                for i in range(13):
                    if i < 12 and i % 3 == 0:
                        act.wait_ge(S1["at_raw"], n(p * 12 + i + 1))
                        act.wait_ge(S1["av_done"], n(p * 8 + 2 * (i // 3) - 2))
                        nc.scalar.copy(pt[1][0:TILE, i % 4], pa1[0:TILE, 0, 0:TOK]).then_inc(S1["off_ready"], 1)
                    yield
                for c in range(4):
                    high(1, p * 7 + 1 + c, ot_hi[1][:, c % 2])
                    yield
                for _ in range(3):
                    yield
                high(1, p * 7 + 5, xt_hi[1][:], vec[:, V_LNG:V_LNG + 1], vec[:, V_LNB:V_LNB + 1])
                yield
                for i in range(TILES):
                    act.wait_ge(S1["qkv_proj"], n(p * 4 + i + 1))
                    nc.scalar.copy(qkv[0:TILE, i], pa1[0:TILE, i % 2, 0:3 * D]).then_inc(S1["qkv_ready"], 1)
                yield
                yield
                yield
                act.wait_ge(S1["qk2_turned"], n(p * 2 + 2))
                nc.scalar.copy(k2t, pa1[:, 1, 0:TOK]).then_inc(S1["k2_ready"], 1)
                yield
                yield
                yield
                for i in range(4):
                    b, hd = i // 2, i % 2
                    act.wait_ge(S1["s2_max"], n(p * 4 + i + 1))
                    for qt, c in ((0, slice(0, TILE)), (1, slice(TILE, 3 * TILE))):
                        last = nc.scalar.activation(p2[i][0:TILE, c], p2[i][0:TILE, c], ACT.Exp,
                                                    bias=row_max[0:TILE, 2 * i + qt:2 * i + qt + 1],
                                                    accum_out=row_sum[0:TILE, 2 * b + qt, hd:hd + 1])
                    last.then_inc(S1["p2_ready"], 1)
                yield
                for i in range(4):
                    act.wait_ge(S1["p2_turned"], n(p * 4 + i + 1))
                    act.wait_ge(S1["pv2_done"], n(p * 4 + i - 1))
                    nc.scalar.copy(fs1[0:TILE, i % 2, 0:3 * TILE],
                                   pa1[0:TILE, 0, 0:3 * TILE]).then_inc(S1["p2t_ready"], 1)
                    yield
                yield
                high(1, p * 7 + 6, ot_hi[1][:, 0])
                yield
                act.wait_ge(S1["y_proj"], n(p + 1))
                nc.scalar.copy(xf_hi[:, 1, 0:TOK], pa1[:, 0, 0:TOK]).then_inc(S1["y_hi"], 1)
                yield
                yield
                gate_exp(1, p)
                yield
                yield
                gate(1, p)
                yield
                yield

            def hidden(kind, p, c):
                _, before = chunks_before(kind, p)
                half = halves_before(kind, p)
                bias = (V_B0, V_B1)[kind] + c
                func = (ACT.Gelu, ACT.Gelu_apprx_tanh)[kind]
                act.wait_ge(F["pre_ready"], n(before + c + 1))
                act.wait_ge(hid_lo_done[c % 2], n(half + (c - HIDS) // 2 + 1))
                nc.scalar.activation(hid[:, c % HIDS], pf[:, c % 2, 0:TOK], func,
                                     bias=vec[:, bias:bias + 1]).then_inc(F["hid_ready"], 1)

            def output(kind, p, j):
                pass

            run_rounds(softmax_queries_and_keys, softmax_attention, linear_and_causal_attention, hidden, output, n)

        @block.vector
        def _(dve):
            n = Counter(dve, "wait_dve")
            dve.wait_ge(started, 1)
            for i in range(PIECES):
                c = slice(i * PIECE, (i + 1) * PIECE)
                dve.wait_ge(w_hi_done, i + 1)
                nc.vector.tensor_tensor(w_lo[:, c], staging[i % 2], w_hi[:, c], ALU.subtract).then_inc(w_lo_done, 1)
            dve.wait_ge(small_loaded, 48)
            nc.vector.tensor_tensor(q_bias[:], vec[:, V_BQ:V_BQ + 1], vec[:, V_OCR:V_OCR + 1],
                                    ALU.add).then_inc(derived, 1)
            nc.vector.scalar_tensor_tensor(qk_gain[:], vec[:, V_QN:V_QN + 1], float(HEAD2) ** 0.5,
                                           vec[:, V_KN:V_KN + 1], ALU.mult, ALU.mult).then_inc(derived, 1)
            dve.wait_ge(derived, 2)

            def low_of_input(k, u):
                p = k * 2 + u
                dve.wait_ge(T["x_hi_done"], n(p + 1))
                nc.vector.tensor_tensor(xf_lo[0:CHANNELS, u], pf[0:CHANNELS, u], xf_hi[0:CHANNELS, u],
                                        ALU.subtract).then_inc(T["x_lo_done"], 1)

            def stats(k, u):
                p = k * 2 + u
                dve.wait_ge(T["y_ready"], n(p + 1))
                nc.vector.bn_stats(bn_part[:, bass.ds(n.index(p * 6), 6)], y_tile[u]).then_inc(T["y_stats"], 1)

            low_of_input(0, 0)
            with n.loop(PAIRS // 2 - 1) as k:
                low_of_input(k, 1)
                stats(k, 0)
                low_of_input(k + 1, 0)
                stats(k, 1)
            low_of_input(PAIRS // 2 - 1, 1)
            stats(PAIRS // 2 - 1, 0)
            stats(PAIRS // 2 - 1, 1)
            dve.wait_ge(T["y_stats"], n(PAIRS))
            nc.vector.bn_aggr(bn[:], bn_part[:]).then_inc(bn_step, 1)
            dve.wait_ge(bn_step, 1)
            nc.vector.tensor_scalar(bn_var[:], bn[:, 1:2], EPS, None, ALU.add).then_inc(bn_step, 1)
            dve.wait_ge(bn_step, 3)
            nc.vector.tensor_tensor(bn_scale[:], bn_rstd[:], vec[:, V_GAMMA:V_GAMMA + 1], ALU.mult
                                    ).then_inc(bn_step, 1)
            dve.wait_ge(bn_step, 4)
            nc.vector.scalar_tensor_tensor(bn_shift[:], bn[:, 0:1], bn_scale[:, 0:1], vec[:, V_BETA:V_BETA + 1],
                                           ALU.mult, ALU.subtract).then_inc(bn_step, 1)
            dve.wait_ge(bn_step, 5)

            def norm_stats(a, count, h, twice=False):
                S = SS[a]
                for i in range(TILES):
                    last = nc.vector.bn_stats(st[a][0:TILE, i], h[0:TILE, i])
                last.then_inc(S["ln_stats"], 1)
                counted = n(count + 1)
                dve.wait_ge(started, 1)
                dve.wait_ge(S["ln_stats"], counted)
                for i in range(TILES):
                    last = nc.vector.bn_aggr(mv[a][0:TILE, i], st[a][0:TILE, i])
                last.then_inc(S["ln_aggr"], 1)
                dve.wait_ge(S["ln_aggr"], n(count + 1))
                scale, shift = (1.0 + EPS, EPS * EPS) if twice else (1.0, EPS)
                nc.vector.tensor_scalar(ve[a][0:TILE], mv[a][0:TILE, :, 1], scale, shift, ALU.mult,
                                        ALU.add).then_inc(S["var_ready"], 1)

            def norm_apply(a, count, h, t):
                S = SS[a]
                dve.wait_ge(S["rstd_ready"], n(count + 1))
                dve.wait_ge(S["turned"], n(t))
                for i in range(TILES):
                    last = nc.vector.tensor_scalar(xn[a][0:TILE, i], h[0:TILE, i], mv[a][0:TILE, i, 0:1],
                                                   rstd[a][0:TILE, i:i + 1], ALU.subtract, ALU.mult)
                last.then_inc(S["xn_ready"], 1)

            def low(a, t, dst, hi):
                dve.wait_ge(SS[a]["hi_ready"], n(t + 1))
                nc.vector.tensor_tensor(dst, pa[a][:, TURN, 0:TOK], hi, ALU.subtract).then_inc(SS[a]["lo_ready"], 1)

            def spread_queries(a, p):
                for g in range(GROUPS):
                    dve.wait_ge(SS[a]["spread"], n(p * 8 + g + 1))
                    nc.vector.tensor_copy(q16[a][:, g], pa[a][:, g % (3, 2)[a], 0:TOK]).then_inc(SS[a]["q_spread"], 1)

            def wide(ap):
                return ap.unsqueeze(2).to_broadcast([TILE, TILES, EXPERTS])

            def gate_logits(a, p):
                S = SS[a]
                dve.wait_ge(S["logit_ready"], n(p + 1))
                first = (R_G0, R_G1)[a]
                bias = rows[0:TILE, first:first + EXPERTS].unsqueeze(1).to_broadcast([TILE, TILES, EXPERTS])
                logits = pa[a][0:TILE, LOGITS[a], 0:TILES * EXPERTS].rearrange("p (t e) -> p t e", t=TILES)
                nc.vector.tensor_tensor(lg[a][0:TILE], logits, bias, ALU.add).then_inc(S["l_biased"], 1)
                dve.wait_ge(S["l_biased"], n(p + 1))
                nc.vector.tensor_reduce(lmax[a][0:TILE], lg[a][0:TILE], AX.X, ALU.max).then_inc(S["l_max"], 1)
                dve.wait_ge(S["l_max"], n(p + 1))
                nc.vector.tensor_tensor(lg[a][0:TILE], lg[a][0:TILE], wide(lmax[a][0:TILE]),
                                        ALU.subtract).then_inc(S["l_shifted"], 1)

            def gate_softmax(a, p):
                S = SS[a]
                dve.wait_ge(S["l_exp"], n(p + 1))
                nc.vector.tensor_reduce(lsum[a][0:TILE], lge[a][0:TILE], AX.X, ALU.add).then_inc(S["l_sum"], 1)
                dve.wait_ge(S["l_sum"], n(p + 1))
                nc.vector.reciprocal(lmax[a][0:TILE], lsum[a][0:TILE]).then_inc(S["l_rec"], 1)
                dve.wait_ge(S["l_rec"], n(p + 1))
                done = S["gate_ready"] if a else S["probs"]
                nc.vector.tensor_tensor(gates[0:TILE, 1] if a else lg[0][0:TILE], lge[a][0:TILE],
                                        wide(lmax[a][0:TILE]), ALU.mult).then_inc(done, 1)

            def gate_top2(p):
                dve.wait_ge(S0["probs"], n(p + 1))
                mine = lg[0][0:TILE].unsqueeze(3).to_broadcast([TILE, TILES, EXPERTS, EXPERTS])
                other = lg[0][0:TILE].unsqueeze(2).to_broadcast([TILE, TILES, EXPERTS, EXPERTS])
                nc.vector.tensor_tensor(over[0:TILE], other, mine, ALU.is_gt).then_inc(S0["ranks1"], 1)
                nc.vector.tensor_tensor(same[0:TILE], other, mine, ALU.is_equal).then_inc(S0["ranks2"], 1)
                dve.wait_ge(S0["ranks2"], n(p + 1))
                flat = earlier[0:TILE].rearrange("p a b -> p (a b)").unsqueeze(1).to_broadcast(
                    [TILE, TILES, EXPERTS * EXPERTS])
                same_flat = same[0:TILE].rearrange("p t a b -> p t (a b)")
                nc.vector.tensor_tensor(same_flat, same_flat, flat, ALU.mult).then_inc(S0["ranks3"], 1)
                dve.wait_ge(S0["ranks3"], n(p + 1))
                nc.vector.tensor_tensor(over[0:TILE], over[0:TILE], same[0:TILE], ALU.add).then_inc(S0["ranks4"], 1)
                dve.wait_ge(S0["ranks4"], n(p + 1))
                nc.vector.tensor_reduce(lge[0][0:TILE], over[0:TILE], AX.X, ALU.add).then_inc(S0["ranks5"], 1)
                dve.wait_ge(S0["ranks5"], n(p + 1))
                nc.vector.scalar_tensor_tensor(gates[0:TILE, 0], lge[0][0:TILE], 2.0, lg[0][0:TILE], ALU.is_lt,
                                               ALU.mult).then_inc(S0["gate_ready"], 1)

            def add_bias2(a, p, h_in, h_out):
                dve.wait_ge(SS[a]["bias2_ready"], n(p + 1))
                nc.vector.tensor_tensor(h_out[0:TILE], by_tile(pa[a][:, BIAS2[a]]), h_in[0:TILE],
                                        ALU.add).then_inc(SS[a]["h_biased"], 1)

            def softmax_queries_and_keys(p):
                dve.wait_ge(y_loaded, n.plain((p + 1) * 16))
                dve.wait_ge(S0["pv_done"], n(p * 16))
                nc.vector.tensor_scalar(z, y_in[:], bn_scale[:, 0:1],
                                        bn_shift[:, 0:1], ALU.mult, ALU.subtract).then_inc(S0["z_ready"], 1)
                yield
                yield
                yield
                dve.wait_ge(S0["h_ready"], n(p + 1))
                norm_stats(0, p * 2, ha)
                yield
                norm_apply(0, p * 2, ha, p * 3)
                yield
                low(0, p * 3, xt_lo[0][:], xt_hi[0][:])
                yield
                dve.wait_ge(S0["qk_hi_ready"], n(p * 2 + 1))
                nc.vector.scalar_tensor_tensor(qk_lo[0][:, 0], pa0[:, 0, 0:TOK], q_bias[:, 0:1], qk_hi[0][:, 0],
                                               ALU.add, ALU.subtract).then_inc(S0["qk_lo_ready"], 1)
                dve.wait_ge(S0["qk_hi_ready"], n(p * 2 + 2))
                nc.vector.scalar_tensor_tensor(qk_lo[0][:, 1], pa0[:, 2, 0:TOK], vec[:, V_BK:V_BK + 1],
                                               qk_hi[0][:, 1], ALU.add, ALU.subtract).then_inc(S0["qk_lo_ready"], 1)
                dve.wait_ge(S0["v_proj"], n(p + 1))
                bv = rows[0:TILE, R_BV:R_BV + D].rearrange("p (h d) -> p h d", h=HEADS)
                for i in range(TILES):
                    last = nc.vector.tensor_tensor(v0[0:TILE, i, :, 0:HEAD],
                                                   pa0[0:TILE, 1, i * D:(i + 1) * D].rearrange(
                                                       "p (h d) -> p h d", h=HEADS), bv, ALU.add)
                last.then_inc(S0["v_ready"], 1)
                yield
                spread_queries(0, p)
                yield
                yield
            def softmax_attention(p):
                for i in range(16):
                    if i and i % 2 == 0:
                        yield
                    b, hd = i // HEADS, i % HEADS
                    dve.wait_ge(S0["s_raw"], n(p * 16 + i + 1))
                    nc.vector.tensor_reduce(minus_max[0:TILE, 2 * b:2 * b + 2, hd // 2, 64 * (hd % 2) + 48],
                                            pa0[0:TILE, i % 3, 0:TOK].rearrange("p (t k) -> p t k", t=2),
                                            AX.X, ALU.max, negate=True).then_inc(S0["s_max"], 1)
                yield
                for g in range(GROUPS):
                    dve.wait_ge(S0["max_turned"], n(p * 4 + g + 1))
                    nc.vector.tensor_tensor(q16[0][:, g], pa0[:, g % 3, 0:TOK], q16[0][:, g],
                                            ALU.add).then_inc(S0["q_shifted"], 1)
                yield
                yield

                def divide(b):
                    dve.wait_ge(S0["pv_done"], n(p * 16 + 8 * b + 8))
                    o = pa0[0:TILE, 2, 0:2 * HEADS * (HEAD + 1)].rearrange("p (t d) -> p t d", d=HEAD + 1)
                    nc.vector.reciprocal(rec[0:TILE, b], o[:, :, HEAD]).then_inc(S0["o_rec"], 1)
                    dve.wait_ge(S0["o_rec"], n(p * 2 + b + 1))
                    nc.vector.tensor_tensor(
                        xn[0][0:TILE, 2 * b:2 * b + 2].rearrange("p t (h d) -> p (t h) d", d=HEAD), o[:, :, 0:HEAD],
                        rec[0:TILE, b].unsqueeze(2).to_broadcast([TILE, 16, HEAD]), ALU.mult
                    ).then_inc(S0["o_ready"], 1)

                for _ in range(4):
                    yield
                divide(0)
                for _ in range(4):
                    yield
                divide(1)
                yield
                yield
                low(0, p * 3 + 1, ot_lo[0][:, 0], ot_hi[0][:, 0])
                yield
                yield
                dve.wait_ge(S0["wo_ready"], n(p + 1))
                dve.wait_ge(S0["h_bo"], n(p + 1))
                nc.vector.tensor_tensor(ha[0:TILE], by_tile(pa0[:, 0]), ha[0:TILE], ALU.add).then_inc(S0["h_attn"], 1)
                dve.wait_ge(S0["h_attn"], n(p + 1))
                norm_stats(0, p * 2 + 1, ha)
                yield
                norm_apply(0, p * 2 + 1, ha, p * 3 + 2)
                yield
                low(0, p * 3 + 2, xf_lo[:, 0, 0:TOK], xf_hi[:, 0, 0:TOK])
                yield
                gate_logits(0, p)
                yield
                yield
                gate_softmax(0, p)
                yield
                gate_top2(p)
                yield
                yield
                dve.wait_ge(S1["carried"], n(p))
                dve.wait_ge(S1["xn_ready"], n(p * 2 - 1))
                add_bias2(0, p, ha, h0)
                yield
                yield

            def linear_and_causal_attention(p):
                first, _ = chunks_before(0, p)
                dve.wait_ge(F["gated"], n(first + EXPERTS))
                norm_stats(1, p * 2, h0)
                yield
                norm_apply(1, p * 2, h0, p * 7)
                yield
                low(1, p * 7, xt_lo[1][:], xt_hi[1][:])
                yield
                yield
                for j in range(2):
                    c = p * 2 + j + 1
                    dve.wait_ge(S1["el_exp"], n(c))
                    nc.vector.tensor_scalar(ts[1][:, 0:TOK], fs1[:, j, 0:TOK], 1.0, None, ALU.min
                                            ).then_inc(S1["el_min"], 1)
                    dve.wait_ge(S1["el_min"], n(c))
                    nc.vector.scalar_tensor_tensor(fs1[:, j, 0:TOK], pa1[:, j, 0:TOK], 0.0, ts[1][:, 0:TOK],
                                                   ALU.max, ALU.add).then_inc(S1["el_map"], 1)
                    dve.wait_ge(S1["el_map"], n(c))
                    nc.vector.tensor_copy(qk_hi[1][:, j], fs1[:, j, 0:TOK]).then_inc(S1["el_hi"], 1)
                    dve.wait_ge(S1["el_hi"], n(c))
                    nc.vector.tensor_tensor(qk_lo[1][:, j], fs1[:, j, 0:TOK], qk_hi[1][:, j],
                                            ALU.subtract).then_inc(S1["el_lo"], 1)
                    yield
                yield
                spread_queries(1, p)
                yield
                yield

                def divide(g8):
                    b, odd, g = g8 // 4, g8 // 2 % 2, g8 % 2
                    dve.wait_ge(S1["av_done"], n(p * 8 + g8 + 1))
                    bank = pa1[0:TILE, 1, 0:4 * (LIN_VALUE + 1)].rearrange("p (h t d) -> p h t d", h=2, t=2)
                    dve.wait_ge(S1["o1_norm"], n(p * 8 + g8))
                    nc.vector.tensor_scalar(den[0:TILE, g8 % 2].rearrange("p (h t) -> p h t", h=2),
                                            bank[:, :, :, LIN_VALUE], 1e-6, None, ALU.max).then_inc(S1["den_done"], 1)
                    dve.wait_ge(S1["den_done"], n(p * 8 + g8 + 1))
                    nc.vector.reciprocal(inv_den[0:TILE, g8 % 2], den[0:TILE, g8 % 2]).then_inc(S1["den_rec"], 1)
                    dve.wait_ge(S1["den_rec"], n(p * 8 + g8 + 1))
                    inv = inv_den[0:TILE, g8 % 2].rearrange("p (h t) -> p h t", h=2).unsqueeze(3).to_broadcast(
                        [TILE, 2, 2, LIN_VALUE])
                    dst = o1[0:TILE, 2 * b:2 * b + 2].rearrange("p t (h r) d -> p h t r d", r=2)[
                        :, 2 * g:2 * g + 2, :, odd]
                    nc.vector.tensor_tensor(dst, bank[:, :, :, 0:LIN_VALUE], inv, ALU.mult
                                            ).then_inc(S1["o1_norm"], 1)

                for i in range(13):
                    if i < 12 and i % 3:
                        before = 2 * (i // 3) - (i % 3 - 1)
                        dve.wait_ge(S1["at_raw"], n(p * 12 + i + 1))
                        dve.wait_ge(S1["av_done"], n(p * 8 + before))
                        nc.vector.tensor_tensor(pt[1][0:TILE, i % 4].rearrange("p (t q) -> p t q", t=4),
                                                pa1[0:TILE, 0, 0:TOK].rearrange("p (t q) -> p t q", t=4),
                                                causal[0:TILE, 0].unsqueeze(1).to_broadcast([TILE, 4, TILE]),
                                                ALU.mult).then_inc(S1["at_ready"], 1)
                    if (i - 1) % 3 and i > 1:
                        divide(2 * ((i - 1) // 3) + (i - 1) % 3 - 1)
                    yield
                for c in range(4):
                    low(1, p * 7 + 1 + c, ot_lo[1][:, c % 2], ot_hi[1][:, c % 2])
                    yield
                yield
                dve.wait_ge(S1["wo1_ready"], n(p + 1))
                dve.wait_ge(S1["carried"], n(p + 1))
                nc.vector.tensor_tensor(h1[0:TILE], by_tile(pa1[:, 0]), h1[0:TILE], ALU.add).then_inc(S1["h_lin"], 1)
                dve.wait_ge(S1["h_lin"], n(p + 1))
                norm_stats(1, p * 2 + 1, h1, True)
                yield
                norm_apply(1, p * 2 + 1, h1, p * 7 + 5)
                yield
                dve.wait_ge(S1["hi_ready"], n(p * 7 + 6))
                nc.vector.tensor_scalar(fs1[:, 0, 0:TOK], pa1[:, TURN, 0:TOK], vec[:, V_LNG:V_LNG + 1],
                                        vec[:, V_LNB:V_LNB + 1], ALU.mult, ALU.add).then_inc(S1["aff_ready"], 1)
                dve.wait_ge(S1["aff_ready"], n(p + 1))
                nc.vector.tensor_tensor(xt_lo[1][:], fs1[:, 0, 0:TOK], xt_hi[1][:],
                                        ALU.subtract).then_inc(S1["lo_ready"], 1)
                yield
                yield
                dve.wait_ge(S1["sq_ready"], n(p + 1))
                nc.vector.tensor_reduce(ss[0:TILE].rearrange("p (t c) -> p t c", t=TILES),
                                        squares[0:TILE].rearrange("p t (c d) -> p t c d", d=HEAD2), AX.X,
                                        ALU.add).then_inc(S1["ss_sum"], 1)
                dve.wait_ge(S1["ss_sum"], n(p + 1))
                nc.vector.tensor_scalar(ss_eps[0:TILE], ss[0:TILE], 1e-12, None, ALU.add).then_inc(S1["ss_ready"], 1)
                yield
                dve.wait_ge(S1["rn_ready"], n(p + 1))
                heads = qkv[0:TILE, :, 0:2 * D].rearrange("p t (c d) -> p t c d", d=HEAD2)
                inv = inv_norm[0:TILE].rearrange("p (t c) -> p t c", t=TILES).unsqueeze(3).to_broadcast(
                    [TILE, TILES, 4, HEAD2])
                nc.vector.tensor_tensor(heads, heads, inv, ALU.mult).then_inc(S1["qkn_ready"], 1)
                yield
                dve.wait_ge(S1["qk2_turned"], n(p * 2 + 1))
                nc.vector.tensor_scalar(q2t, pa1[:, 0, 0:TOK], qk_gain[:, 0:1], None, ALU.mult
                                        ).then_inc(S1["q2_ready"], 1)
                yield
                for i in range(4):
                    dve.wait_ge(S1["s2_raw"], n(p * 4 + i + 1))
                    nc.vector.tensor_tensor(p2[i][0:TILE, 0:3 * TILE], pa1[0:TILE, i % 2, 0:3 * TILE],
                                            causal_add[0:TILE].rearrange("p a b -> p (a b)"),
                                            ALU.add).then_inc(S1["s2_masked"], 1)
                    dve.wait_ge(S1["s2_masked"], n(p * 4 + i + 1))
                    for qt, c in ((0, slice(0, TILE)), (1, slice(TILE, 3 * TILE))):
                        last = nc.vector.tensor_reduce(row_max[0:TILE, 2 * i + qt:2 * i + qt + 1],
                                                       p2[i][0:TILE, c], AX.X, ALU.max, negate=True)
                    last.then_inc(S1["s2_max"], 1)
                    if i % 2 == 1:
                        yield
                for _ in range(5):
                    yield
                dve.wait_ge(S1["pv2_done"], n(p * 4 + 4))
                nc.vector.reciprocal(inv_sum[0:TILE], row_sum[0:TILE].rearrange("p t h -> p (t h)")
                                     ).then_inc(S1["rs_rec"], 1)
                dve.wait_ge(S1["rs_rec"], n(p + 1))
                nc.vector.tensor_tensor(
                    xn[1][0:TILE].rearrange("p t (h d) -> p (t h) d", d=HEAD2),
                    pa1[0:TILE, 1].rearrange("p (c d) -> p c d", d=HEAD2),
                    inv_sum[0:TILE].unsqueeze(2).to_broadcast([TILE, 8, HEAD2]), ALU.mult
                ).then_inc(S1["o2_ready"], 1)
                yield
                low(1, p * 7 + 6, ot_lo[1][:, 0], ot_hi[1][:, 0])
                yield
                dve.wait_ge(S1["y_hi"], n(p + 1))
                nc.vector.tensor_tensor(xf_lo[:, 1, 0:TOK], pa1[:, 0, 0:TOK], xf_hi[:, 1, 0:TOK],
                                        ALU.subtract).then_inc(S1["y_lo"], 1)
                yield
                gate_logits(1, p)
                yield
                yield
                gate_softmax(1, p)
                yield
                yield
                dve.wait_ge(out_sent, n.plain(p * 32))
                add_bias2(1, p, h1, h2)
                yield

            def hidden(kind, p, c):
                _, before = chunks_before(kind, p)
                dve.wait_ge(F["hid_ready"], n(before + c + 1))
                dve.wait_ge(F["hid_used"], n(before + c - 7))
                nc.vector.tensor_copy(hid_hi[:, c % 8], hid[:, c % HIDS]).then_inc(F["hid_hi_done"], 1)
                if c % 2 == 0 and not POOL_EVEN:
                    dve.wait_ge(F["hid_hi_done"], n(before + c + 1))
                    nc.vector.tensor_tensor(hid_lo[:, c % 8], hid[:, c % HIDS], hid_hi[:, c % 8],
                                            ALU.subtract).then_inc(hid_lo_done[0], 1)

            def output(kind, p, j):
                experts_before, before = chunks_before(kind, p)
                h = h_of[kind]
                per = (CHUNKS0, CHUNKS1)[kind]
                e, m = j // per, j % per
                if m == per - 1:
                    dve.wait_ge(F["hid_used"], n(before + (e + 1) * per))
                    if e == 0:
                        dve.wait_ge(SS[kind]["h_biased"], n(p + 1))
                    dve.wait_ge(F["gated"], n(experts_before + e))
                    for i in range(TILES):
                        last = nc.vector.scalar_tensor_tensor(
                            h[0:TILE, i], pf[0:TILE, 2, i * D:(i + 1) * D],
                            gates[0:TILE, kind, i, e:e + 1], h[0:TILE, i], ALU.mult, ALU.add)
                    last.then_inc(F["gated"], 1)

            run_rounds(softmax_queries_and_keys, softmax_attention, linear_and_causal_attention, hidden, output, n)

        @block.tensor
        def _(pe):
            n = Counter(pe, "wait_pe")

            def mm3(out, a, b, start=True, stop=True, skip=False):
                (ah, al), (bh, bl) = a, b
                nc.tensor.matmul(out, ah, bh, start=start, stop=False, skip_group_check=skip)
                nc.tensor.matmul(out, ah, bl, start=False, stop=False, skip_group_check=skip)
                return nc.tensor.matmul(out, al, bh, start=False, stop=stop, skip_group_check=skip)

            pe.wait_ge(started, 1)
            pe.wait_ge(consts_built, 1)
            pe.wait_ge(w_lo_done, 1)

            def turn_input(k, u):
                p = k * 2 + u
                pe.wait_ge(x_loaded[u], n.plain((k + 1) * 32))
                pe.wait_ge(T["x_lo_done"], n(p - 1))
                for i in range(4):
                    last = nc.tensor.transpose(pf[0:CHANNELS, u, i * 128:(i + 1) * 128],
                                               x_in[u][:, i * CHANNELS:(i + 1) * CHANNELS], ident[:])
                last.then_inc(T["x_turned"], 1)

            def taps(k, u):
                p = k * 2 + u
                pe.wait_ge(T["x_lo_done"], n(p + 1))
                pe.wait_ge(T["y_ready"], n(p - 1))
                for c in range(TAPS):
                    xs = [v[0:CHANNELS, u, :].rearrange("p (b l) -> p b l", b=2)[:, :, c:c + SEQ]
                          for v in (xf_hi, xf_lo)]
                    last = mm3(pa0[:, u, 0:TOK].rearrange("p (b l) -> p b l", b=2), W("tok", c * D, D, CHANNELS),
                               xs, c == 0, c == TAPS - 1)
                last.then_inc(T["y_pre"], 1)

            turn_input(0, 0)
            with n.loop(PAIRS // 2 - 1) as k:
                turn_input(k, 1)
                taps(k, 0)
                turn_input(k + 1, 0)
                taps(k, 1)
            turn_input(PAIRS // 2 - 1, 1)
            taps(PAIRS // 2 - 1, 0)
            taps(PAIRS // 2 - 1, 1)

            def turn(a, t, src):
                pe.wait_ge(SS[a]["hi_ready"], n(t))
                pe.wait_ge(SS[a]["lo_ready"], n(t))
                for i in range(TILES):
                    last = nc.tensor.transpose(pa[a][:, TURN, cols(i)], src[0:TILE, i], ident[0:TILE, 0:TILE])
                last.then_inc(SS[a]["turned"], 1)

            def halves_ready(a, t):
                pe.wait_ge(SS[a]["hi_ready"], n(t + 1))
                pe.wait_ge(SS[a]["lo_ready"], n(t + 1))

            def spread_queries(a, p):
                for g in range(GROUPS):
                    banks = (3, 2)[a]
                    if g >= banks:
                        pe.wait_ge(SS[a]["q_spread"], n(p * 4 + g - banks + 1))
                    nc.tensor.matmul(pa[a][:, g % banks, 0:TOK], pick_q_hi[:, g], qk_hi[a][:, 0], start=True, stop=False)
                    nc.tensor.matmul(pa[a][:, g % banks, 0:TOK], pick_q_lo[:, g], qk_lo[a][:, 0], start=False,
                                     stop=True).then_inc(SS[a]["spread"], 1)

            def spread_keys(a, p):
                for g in range(GROUPS):
                    banks = (3, 2)[a]
                    bank = (GROUPS + g) % banks
                    if g < banks:
                        pe.wait_ge(SS[a]["q_spread"], n(p * 4 + min(GROUPS + g - banks + 1, GROUPS)))
                    else:
                        pe.wait_ge(SS[a]["k_spread"], n(p * 4 + g - banks + 1))
                    nc.tensor.matmul(pa[a][:, bank, 0:TOK], pick_k_hi[:, g], qk_hi[a][:, 1], start=True, stop=False)
                    nc.tensor.matmul(pa[a][:, bank, 0:TOK], pick_k_lo[:, g], qk_lo[a][:, 1], start=False,
                                     stop=True).then_inc(SS[a]["spread"], 1)

            def gate_logits(a, p):
                for i in range(TILES):
                    xs = (xf_hi[:, a, cols(i)], xf_lo[:, a, cols(i)])
                    last = mm3(pa[a][0:TILE, LOGITS[a], i * EXPERTS:(i + 1) * EXPERTS], xs,
                               W(("gate0", "gate1")[a], 0, EXPERTS))
                last.then_inc(SS[a]["logit_ready"], 1)

            def gate_turn(a, p):
                pe.wait_ge(SS[a]["gate_ready"], n(p + 1))
                for i in range(TILES):
                    last = nc.tensor.transpose(pa[a][0:EXPERTS, GATES_T[a], cols(i)], gates[0:TILE, a, i],
                                               ident[0:TILE, 0:TILE])
                last.then_inc(SS[a]["gate_turned"], 1)

            def gate_bias2(a, p):
                pe.wait_ge(SS[a]["gate_t_ready"], n(p + 1))
                for i in range(TILES):
                    last = nc.tensor.matmul(pa[a][0:TILE, BIAS2[a], i * D:(i + 1) * D], gate_t[a][:, cols(i)],
                                            b2[:, a], start=True, stop=True)
                last.then_inc(SS[a]["bias2_ready"], 1)

            def softmax_queries_and_keys(p):
                yield
                yield
                yield
                pe.wait_ge(S0["z_ready"], n(p + 1))
                pe.wait_ge(S0["h_biased"], n(p))
                for i in range(TILES):
                    last = nc.tensor.transpose(pa0[0:TILE, 0, i * D:(i + 1) * D], z[:, cols(i)], ident[:])
                last.then_inc(S0["z_turned"], 1)
                yield
                yield
                pe.wait_ge(S0["xn_ready"], n(p * 2 + 1))
                turn(0, p * 3, xn[0])
                yield
                halves_ready(0, p * 3)
                xt = (xt_hi[0][:], xt_lo[0][:])
                pe.wait_ge(S0["h_ready"], n(p + 1))
                mm3(pa0[:, 0, 0:TOK], W("wq0", 0, D), xt).then_inc(S0["q_proj"], 1)
                mm3(pa0[:, 2, 0:TOK], W("wk0", 0, D), xt).then_inc(S0["k_proj"], 1)
                for i in range(TILES):
                    last = mm3(pa0[0:TILE, 1, i * D:(i + 1) * D],
                               (xt_hi[0][:, cols(i)], xt_lo[0][:, cols(i)]), W("wv0", 0, D))
                last.then_inc(S0["v_proj"], 1)
                yield
                pe.wait_ge(S0["qk_lo_ready"], n(p * 2 + 2))
                pe.wait_ge(S0["v_ready"], n(p + 1))
                spread_queries(0, p)
                yield
                spread_keys(0, p)
                yield
            def softmax_attention(p):
                pe.wait_ge(S0["k_spread"], n(p * 4 + 4))
                for i in range(16):
                    if i and i % 2 == 0:
                        yield
                    b, hd = i // HEADS, i % HEADS
                    if i >= 3:
                        pe.wait_ge(S0["s_max"], n(p * 16 + i - 2))
                    for j in range(2):
                        last = nc.tensor.matmul(pa0[0:TILE, i % 3, j * SEQ:(j + 1) * SEQ],
                                                q16[0][head_rows(hd), hd // 2, cols(2 * b + j)],
                                                k16[0][head_rows(hd), hd // 2, b * SEQ:(b + 1) * SEQ],
                                                start=True, stop=True)
                    last.then_inc(S0["s_raw"], 1)
                yield
                pe.wait_ge(S0["s_max"], n(p * 16 + 16))
                for g in range(GROUPS):
                    if g >= 3:
                        pe.wait_ge(S0["q_shifted"], n(p * 4 + g - 2))
                    for i in range(TILES):
                        last = nc.tensor.matmul(pa0[:, g % 3, cols(i)], minus_max[0:TILE, i, g],
                                                ident16[0:TILE, 0:TILE], start=True, stop=True)
                    last.then_inc(S0["max_turned"], 1)
                yield

                def scores(i):
                    b, hd = i // HEADS, i % HEADS
                    if i >= 2:
                        pe.wait_ge(S0["p_exp"], n(p * 16 + i - 1))
                    for j in range(2):
                        last = nc.tensor.matmul(pa0[0:TILE, i % 2, j * SEQ:(j + 1) * SEQ],
                                                k16[0][head_rows(hd), hd // 2, cols(2 * b + j)],
                                                q16[0][head_rows(hd), hd // 2, b * SEQ:(b + 1) * SEQ],
                                                start=True, stop=True)
                    last.then_inc(S0["st_ready"], 1)

                def values(i):
                    b, hd = i // HEADS, i % HEADS
                    pe.wait_ge(S0["p_band"], n(p * 16 + i + 1))
                    if i == 8:
                        pe.wait_ge(S0["o_ready"], n(p * 2 + 1))
                    for j in range(2):
                        first = (j * HEADS + hd) * (HEAD + 1)
                        for kt in range(2):
                            c0 = kt * SEQ + j * TILE
                            last = nc.tensor.matmul(pa0[0:TILE, 2, first:first + HEAD + 1],
                                                    pt[0][0:TILE, i % 8, c0:c0 + TILE],
                                                    v0[0:TILE, 2 * b + kt, hd], start=(kt == 0), stop=(kt == 1))
                    last.then_inc(S0["pv_done"], 1)

                pe.wait_ge(S0["q_shifted"], n(p * 4 + 4))
                for g in range(10):
                    for i in (2 * g - 4, 2 * g - 3):
                        if g >= 2:
                            values(i)
                    for i in (2 * g, 2 * g + 1):
                        if g < 8:
                            scores(i)
                    yield
                yield
                pe.wait_ge(S0["o_ready"], n(p * 2 + 2))
                turn(0, p * 3 + 1, xn[0])
                yield
                halves_ready(0, p * 3 + 1)
                for i in range(TILES):
                    last = mm3(pa0[0:TILE, 0, i * D:(i + 1) * D],
                               (ot_hi[0][:, 0, cols(i)], ot_lo[0][:, 0, cols(i)]), W("wo0", 0, D))
                last.then_inc(S0["wo_ready"], 1)
                yield
                yield
                yield
                pe.wait_ge(S0["xn_ready"], n(p * 2 + 2))
                turn(0, p * 3 + 2, xn[0])
                yield
                halves_ready(0, p * 3 + 2)
                gate_logits(0, p)
                yield
                yield
                yield
                yield
                gate_turn(0, p)
                yield
                gate_bias2(0, p)
                yield
                yield

            def linear_and_causal_attention(p):
                yield
                yield
                pe.wait_ge(S1["xn_ready"], n(p * 2 + 1))
                pe.wait_ge(S1["h_biased"], n(p))
                turn(1, p * 7, xn[1])
                yield
                halves_ready(1, p * 7)
                xt = (xt_hi[1][:], xt_lo[1][:])
                mm3(pa1[:, 0, 0:TOK], W("wq1", 0, D), xt).then_inc(S1["q_proj"], 1)
                mm3(pa1[:, 1, 0:TOK], W("wk1", 0, D), xt).then_inc(S1["k_proj"], 1)
                yield
                yield
                for tiles in ((0,), (1, 2), (3,)):
                    for i in tiles:
                        if i < 2:
                            pe.wait_ge(S1["el_map"], n(p * 2 + i + 1))
                        else:
                            pe.wait_ge(S1["v1_ready"], n(p * 4 + i - 1))
                        mm3(pa1[0:TILE, i % 2, 0:HEADS * LIN_VALUE],
                            (xt_hi[1][:, cols(i)], xt_lo[1][:, cols(i)]),
                            W("wv1", 0, HEADS * LIN_VALUE)).then_inc(S1["v1_proj"], 1)
                    if i < 3:
                        yield
                pe.wait_ge(S1["el_lo"], n(p * 2 + 2))
                pe.wait_ge(S1["v1_ready"], n(p * 4 + 4))
                spread_queries(1, p)
                yield
                spread_keys(1, p)
                yield
                pe.wait_ge(S1["k_spread"], n(p * 4 + 4))
                for i in range(13):
                    if i < 12:
                        quad, part = i // 3, i % 3
                        b = quad // 2
                        if part == 1:
                            pe.wait_ge(S1["off_ready"], n(p * 4 + quad + 1))
                        elif i:
                            pe.wait_ge(S1["at_ready"], n(p * 8 + 2 * quad + part // 2))
                        for blk in range(4):
                            if part == 0:
                                hd, kt, qt = 2 * blk + quad % 2, 0, 1
                            else:
                                hd, kt, qt = 4 * (part - 1) + 2 * (blk // 2) + quad % 2, blk % 2, blk % 2
                            last = nc.tensor.matmul(pa1[0:TILE, 0, cols(blk)],
                                                    k16[1][head_rows(hd), hd // 2, cols(2 * b + kt)],
                                                    q16[1][head_rows(hd), hd // 2, cols(2 * b + qt)],
                                                    start=True, stop=True)
                        last.then_inc(S1["at_raw"], 1)
                    if (i - 1) % 3 and i > 1:
                        quad, part = (i - 1) // 3, (i - 1) % 3
                        g8 = 2 * quad + part - 1
                        b, wide = quad // 2, LIN_VALUE + 1
                        pe.wait_ge(S1["at_ready"], n(p * 8 + g8 + 1))
                        pe.wait_ge(S1["o1_norm"], n(p * 8 + g8))
                        off, diagonal = pt[1][0:TILE, 3 * quad % 4], pt[1][0:TILE, (i - 1) % 4]
                        for m in range(2):
                            hd = 4 * (part - 1) + 2 * m + quad % 2
                            for qt, terms in ((0, ((0, diagonal, 2 * m),)),
                                              (1, ((0, off, hd // 2), (1, diagonal, 2 * m + 1)))):
                                first = (2 * m + qt) * wide
                                for t, (kt, factors, blk) in enumerate(terms):
                                    last = nc.tensor.matmul(pa1[0:TILE, 1, first:first + wide], factors[:, cols(blk)],
                                                            v1[0:TILE, 2 * b + kt, hd], start=(t == 0),
                                                            stop=(t == len(terms) - 1))
                        last.then_inc(S1["av_done"], 1)
                    yield
                for c in range(5):
                    if c < 4:
                        if c == 0:
                            pe.wait_ge(S1["o1_norm"], n(p * 8 + 8))
                        turn(1, p * 7 + 1 + c, o1_rows[:, :, c * 128:(c + 1) * 128])
                    if c >= 1:
                        halves_ready(1, p * 7 + c)
                        for i in range(TILES):
                            last = mm3(pa1[0:TILE, 0, i * D:(i + 1) * D],
                                       (ot_hi[1][:, (c - 1) % 2, cols(i)], ot_lo[1][:, (c - 1) % 2, cols(i)]),
                                       W("wo1", (c - 1) * D, D), c == 1 and i == 0, c == 4 and i == 3, True)
                    if c == 4:
                        last.then_inc(S1["wo1_ready"], 1)
                    yield
                yield
                yield
                pe.wait_ge(S1["xn_ready"], n(p * 2 + 2))
                turn(1, p * 7 + 5, xn[1])
                yield
                halves_ready(1, p * 7 + 5)
                for i in range(TILES):
                    if i >= 2:
                        pe.wait_ge(S1["qkv_ready"], n(p * 4 + i - 1))
                    mm3(pa1[0:TILE, i % 2, 0:3 * D], (xt_hi[1][:, cols(i)], xt_lo[1][:, cols(i)]),
                        W("wqkv2", 0, 3 * D)).then_inc(S1["qkv_proj"], 1)
                yield
                yield
                yield
                pe.wait_ge(S1["qkn_ready"], n(p + 1))
                for j in range(2):
                    for i in range(TILES):
                        last = nc.tensor.transpose(pa1[:, j, cols(i)], qkv[0:TILE, i, j * D:(j + 1) * D],
                                                   ident[0:TILE, 0:TILE])
                    last.then_inc(S1["qk2_turned"], 1)
                yield
                pe.wait_ge(S1["q2_ready"], n(p + 1))
                pe.wait_ge(S1["k2_ready"], n(p + 1))
                for i in range(4):
                    b, hd = i // 2, i % 2
                    if i >= 2:
                        pe.wait_ge(S1["s2_masked"], n(p * 4 + i - 1))
                    bank = pa1[0:TILE, i % 2]
                    nc.tensor.matmul(bank[:, 0:TILE], q2t[head_rows(hd), cols(2 * b)],
                                     k2t[head_rows(hd), cols(2 * b)], start=True, stop=True)
                    nc.tensor.matmul(bank[:, TILE:3 * TILE], q2t[head_rows(hd), cols(2 * b + 1)],
                                     k2t[head_rows(hd), b * SEQ:(b + 1) * SEQ], start=True,
                                     stop=True).then_inc(S1["s2_raw"], 1)
                    if i % 2 == 1:
                        yield
                yield
                for i in range(5):
                    if i < 4:
                        pe.wait_ge(S1["p2_ready"], n(p * 4 + i + 1))
                        pe.wait_ge(S1["s2_masked"], n(p * 4 + 4))
                        pe.wait_ge(S1["p2t_ready"], n(p * 4 + i))
                        for blk in range(3):
                            last = nc.tensor.transpose(pa1[0:TILE, 0, cols(blk)], p2[i][0:TILE, cols(blk)],
                                                       ident[0:TILE, 0:TILE])
                        last.then_inc(S1["p2_turned"], 1)
                    if i >= 1:
                        j = i - 1
                        b, hd = j // 2, j % 2
                        pe.wait_ge(S1["p2t_ready"], n(p * 4 + j + 1))
                        for qt, blocks in ((0, ((0, 0),)), (1, ((0, 1), (1, 2)))):
                            first = ((2 * b + qt) * HEADS2 + hd) * HEAD2
                            c0 = 2 * D + hd * HEAD2
                            for m, (kt, blk) in enumerate(blocks):
                                last = nc.tensor.matmul(pa1[0:TILE, 1, first:first + HEAD2],
                                                        fs1[0:TILE, j % 2, cols(blk)],
                                                        qkv[0:TILE, 2 * b + kt, c0:c0 + HEAD2], start=(m == 0),
                                                        stop=(m == len(blocks) - 1))
                        last.then_inc(S1["pv2_done"], 1)
                    yield
                pe.wait_ge(S1["o2_ready"], n(p + 1))
                turn(1, p * 7 + 6, xn[1])
                yield
                halves_ready(1, p * 7 + 6)
                mm3(pa1[:, 0, 0:TOK], W("wo2", 0, D), (ot_hi[1][:, 0], ot_lo[1][:, 0])).then_inc(S1["y_proj"], 1)
                yield
                pe.wait_ge(S1["y_hi"], n(p + 1))
                pe.wait_ge(S1["y_lo"], n(p + 1))
                gate_logits(1, p)
                yield
                yield
                yield
                gate_turn(1, p)
                yield
                gate_bias2(1, p)
                yield

            def hidden(kind, p, c):
                _, before = chunks_before(kind, p)
                pe.wait_ge(F["hid_ready"], n(before + c - 1))
                mm3(pf[:, c % 2, 0:TOK], W(("up0", "up1")[kind], c * 128, 128),
                    (xf_hi[:, kind, 0:TOK], xf_lo[:, kind, 0:TOK])).then_inc(F["pre_ready"], 1)

            def output(kind, p, j):
                experts_before, before = chunks_before(kind, p)
                half = halves_before(kind, p)
                per = (CHUNKS0, CHUNKS1)[kind]
                e, m = j // per, j % per
                pe.wait_ge(F["hid_hi_done"], n(before + j + 1))
                pe.wait_ge(hid_lo_done[j % 2], n(half + j // 2 + 1))
                if m == 0:
                    pe.wait_ge(F["gated"], n(experts_before + e))
                for i in range(TILES):
                    last = mm3(pf[0:TILE, 2, i * D:(i + 1) * D],
                               (hid_hi[:, j % 8, cols(i)], hid_lo[:, j % 8, cols(i)]),
                               W(("down0", "down1")[kind], j * D, D), m == 0 and i == 0,
                               m == per - 1 and i == 3, True)
                last.then_inc(F["hid_used"], 1)

            run_rounds(softmax_queries_and_keys, softmax_attention, linear_and_causal_attention, hidden, output, n)


def kernel(**inputs):
    import numpy as _np
    import concourse.bacc as _bacc
    from concourse import mybir as _mybir
    from concourse.bass_utils import run_bass_kernel_spmd as _run

    a = {name: _np.asarray(value) for name, value in inputs.items()}

    def taps_first():
        w = a["L0_tok_W"].reshape(D, TAPS, CHANNELS).transpose(2, 1, 0).reshape(CHANNELS, TAPS * D)
        return _np.concatenate([w, _np.zeros((128 - CHANNELS, TAPS * D), w.dtype)], 0)

    def by_chunk(w):
        e, f, d = w.shape
        return w.reshape(e, f // 128, 128, d).transpose(2, 0, 1, 3).reshape(128, -1)

    def inputs_first(w):
        return w.transpose(1, 0, 2).reshape(D, -1)

    weights = {
        "tok": taps_first(),
        "wq0": a["L0_attn_Wq"].T, "wk0": a["L0_attn_Wk"].T, "wv0": a["L0_attn_Wv"].T, "wo0": a["L0_attn_Wo"].T,
        "wq1": a["L1_attn_W_q"].T, "wk1": a["L1_attn_W_k"].T, "wv1": a["L1_attn_W_v"].T,
        "wo1": a["L1_attn_W_out"].T.reshape(HEADS * LIN_VALUE // 128, 128, D).transpose(1, 0, 2).reshape(128, -1),
        "wqkv2": _np.concatenate([a["L1_ffn_Wq"], a["L1_ffn_Wk"], a["L1_ffn_Wv"]], 1), "wo2": a["L1_ffn_Wo"],
        "gate0": a["L0_ffn_Wr"].T, "gate1": a["L1_ffn_gate_W"],
        "up0": inputs_first(a["L0_ffn_W1"]), "down0": by_chunk(a["L0_ffn_W2"]),
        "up1": inputs_first(a["L1_ffn_W1"]), "down1": by_chunk(a["L1_ffn_W2"]),
    }
    columns = [a["L0_tok_b"], a["L0_tok_gamma"], a["L0_tok_beta"], a["L0_attn_bq"], a["L0_attn_ocr_bias"],
               a["L0_attn_bk"], a["L1_ffn_ln_g"], a["L1_ffn_ln_b"], _np.tile(a["L1_ffn_qn_g"], HEADS2),
               _np.tile(a["L1_ffn_kn_g"], HEADS2), *a["L0_ffn_b1"].reshape(-1, 128), *a["L1_ffn_b1"].reshape(-1, 128)]
    arrays = {
        "x": a["x"],
        "weights": _np.concatenate([weights[name] for name, _ in WIDTHS], 1),
        "vectors": _np.stack(columns, 1),
        "rows": _np.concatenate([a["L0_attn_bv"], a["L0_attn_bo"], a["L0_ffn_br"], a["L1_ffn_gate_b"]]),
        "b2": _np.stack([a["L0_ffn_b2"], a["L1_ffn_b2"]], 1),
    }
    nc = _bacc.Bacc("TRN2", target_bir_lowering=False, num_devices=1)
    arrays = {f"in_{name}": _np.ascontiguousarray(v) for name, v in arrays.items()}
    args = [nc.dram_tensor(name, v.shape, _mybir.dt.from_np(v.dtype), kind="ExternalInput").ap()
            for name, v in arrays.items()]
    args.append(nc.dram_tensor("out", (BATCH, SEQ, D), F32, kind="ExternalOutput").ap())
    program(nc, *args)
    return _run(nc, [arrays], core_ids=[0]).results[0]["out"]
```
